# Optimizing a Trainium2 kernel written in Bass

```python
import numpy as np
import jax
import jax.numpy as jnp

def _softmax(x, axis=-1):
    return jax.nn.softmax(x, axis=axis)

def _gelu(x):
    return jax.nn.gelu(x, approximate=True)

def _silu(x):
    return jax.nn.silu(x)

def _sigmoid(x):
    return jax.nn.sigmoid(x)

def _layernorm(x, axis=-1, eps=1e-05):
    m = jnp.mean(x, axis=axis, keepdims=True)
    v = jnp.var(x, axis=axis, keepdims=True)
    return (x - m) / jnp.sqrt(v + eps)

def _scatter_add(tgt, idx, src, axis=0):
    return tgt.at[idx].add(src)

def _segment_sum(src, seg, n):
    return jax.ops.segment_sum(src, seg, n)
kernel_name = 'mk_flamingo_gated_d1_seqx_r8_32e749'

def setup_inputs(seed: int=0):
    np.random.seed(seed)
    _w = jnp.asarray

    def _rec_inputs():
        import jax
        import jax.numpy as jnp
        _rk = jax.random.key(seed)
        x = 7.22e-05 + 1 * jax.random.normal(jax.random.fold_in(_rk, 1), (16, 256, 128), jnp.float32)
        _lenS = 256 - jax.random.randint(jax.random.fold_in(_rk, 7), (16,), 0, max(1, 256 // 4) + 1, jnp.int32)
        _lenS2 = 64 - jax.random.randint(jax.random.fold_in(_rk, 8), (16,), 0, max(1, 64 // 4) + 1, jnp.int32)
        _ctx_1024P = jax.random.normal(jax.random.fold_in(_rk, 11), (16, 16, 128), jnp.float32)
        _ctx_1024c = jax.random.dirichlet(jax.random.fold_in(_rk, 511), 0.3 * jnp.ones((16,), jnp.float32), (16, 64))
        _ctx_1024t = jnp.einsum('bsk,bkd->bsd', _ctx_1024c, _ctx_1024P)
        _ctx_1024t = _ctx_1024t * jax.lax.rsqrt(jnp.mean(jnp.square(_ctx_1024t)) + 1e-12) * 0.953939
        ctx_1024 = 4.13588e-05 + 0.999923 * (_ctx_1024t + 0.3 * jax.random.normal(jax.random.fold_in(_rk, 611), (16, 64, 128), jnp.float32))
        _validS = jnp.arange(256)[None, :] < _lenS[:, None]
        _validS2 = jnp.arange(64)[None, :] < _lenS2[:, None]
        _causal = jnp.tril(jnp.ones((256, 256), dtype=bool))
        mask_1x1xSxS2_ik0 = jnp.where(jnp.broadcast_to(_validS2[0:1, None, None, :], (1, 1, 256, 64)), 0, 1).astype(jnp.int32)
        _g = jax.random.normal(jax.random.fold_in(_rk, 9001), (2, 1), jnp.float32)
        _g = jnp.sign(_g) * jnp.maximum(jnp.abs(_g), 1.0) + (_g == 0) * 1.0
        g_xattn = _g[0]
        g_ffn = _g[1]
        return (x, ctx_1024, mask_1x1xSxS2_ik0, g_xattn, g_ffn)
    x, ctx_1024, mask_1x1xSxS2_ik0, g_xattn, g_ffn = _rec_inputs()

    def _L0_xattn_setup():
        import jax, jax.numpy as jnp
        import numpy as np
        import math
        D_MODEL = 128
        N_HEADS = 16
        D_K = D_MODEL // N_HEADS
        B, S = (4, 256)
        key = jax.random.key(seed)
        ks = jax.random.split(key, 11)
        sc = 1.0 / math.sqrt(D_MODEL)
        inp = {'q': jax.random.normal(ks[0], (B, S, D_MODEL), jnp.float32), 'k': jax.random.normal(ks[1], (B, S, D_MODEL), jnp.float32), 'v': jax.random.normal(ks[2], (B, S, D_MODEL), jnp.float32), 'mask': jnp.tril(jnp.ones((S, S), jnp.int32))[None, None], 'wq': jax.random.normal(ks[3], (D_MODEL, D_MODEL), jnp.float32) * sc, 'bq': jnp.zeros((D_MODEL,), jnp.float32), 'wk': jax.random.normal(ks[4], (D_MODEL, D_MODEL), jnp.float32) * sc, 'bk': jnp.zeros((D_MODEL,), jnp.float32), 'wv': jax.random.normal(ks[5], (D_MODEL, D_MODEL), jnp.float32) * sc, 'bv': jnp.zeros((D_MODEL,), jnp.float32), 'wo': jax.random.normal(ks[6], (D_MODEL, D_MODEL), jnp.float32) * sc, 'bo': jnp.zeros((D_MODEL,), jnp.float32)}
        return inp
    _L0_xattn_all = _L0_xattn_setup()
    _L0_xattn_in = {k: v for k, v in _L0_xattn_all.items() if k in ('wq', 'bq', 'wk', 'bk', 'wv', 'bv', 'wo', 'bo')}
    del _L0_xattn_all

    def _L0_ffn_setup():
        import jax, jax.numpy as jnp
        import numpy as np
        DIM = 128
        HIDDEN = 512
        E = 8
        B, S = (2, 512)
        key = jax.random.key(seed)
        ks = jax.random.split(key, 8)
        sd = 1.0 / np.sqrt(DIM)
        sh = 1.0 / np.sqrt(HIDDEN)
        return {'x': jax.random.normal(ks[0], (B, S, DIM), dtype=jnp.float32), 'router_w': jax.random.uniform(ks[1], (DIM, E), jnp.float32, -sd, sd), 'router_b': jax.random.uniform(ks[2], (E,), jnp.float32, -sd, sd), 'w1': jax.random.uniform(ks[3], (E, DIM, 2 * HIDDEN), jnp.float32, -sd, sd), 'b1': jax.random.uniform(ks[4], (E, 2 * HIDDEN), jnp.float32, -sd, sd), 'w2': jax.random.uniform(ks[5], (E, HIDDEN, DIM), jnp.float32, -sh, sh), 'b2': jax.random.uniform(ks[6], (E, DIM), jnp.float32, -sh, sh)}
    _L0_ffn_all = _L0_ffn_setup()
    _L0_ffn_in = {k: v for k, v in _L0_ffn_all.items() if k in ('router_w', 'router_b', 'w1', 'b1', 'w2', 'b2')}
    del _L0_ffn_all
    return {'x': x, 'ctx_1024': ctx_1024, 'mask_1x1xSxS2_ik0': mask_1x1xSxS2_ik0, 'g_xattn': g_xattn, 'g_ffn': g_ffn, 'L0_xattn_wq': _L0_xattn_in['wq'], 'L0_xattn_bq': _L0_xattn_in['bq'], 'L0_xattn_wk': _L0_xattn_in['wk'], 'L0_xattn_bk': _L0_xattn_in['bk'], 'L0_xattn_wv': _L0_xattn_in['wv'], 'L0_xattn_bv': _L0_xattn_in['bv'], 'L0_xattn_wo': _L0_xattn_in['wo'], 'L0_xattn_bo': _L0_xattn_in['bo'], 'L0_ffn_router_w': _L0_ffn_in['router_w'], 'L0_ffn_router_b': _L0_ffn_in['router_b'], 'L0_ffn_w1': _L0_ffn_in['w1'], 'L0_ffn_b1': _L0_ffn_in['b1'], 'L0_ffn_w2': _L0_ffn_in['w2'], 'L0_ffn_b2': _L0_ffn_in['b2']}

def reference(x, ctx_1024, mask_1x1xSxS2_ik0, g_xattn, g_ffn, L0_xattn_wq, L0_xattn_bq, L0_xattn_wk, L0_xattn_bk, L0_xattn_wv, L0_xattn_bv, L0_xattn_wo, L0_xattn_bo, L0_ffn_router_w, L0_ffn_router_b, L0_ffn_w1, L0_ffn_b1, L0_ffn_w2, L0_ffn_b2):
    import jax
    import jax.numpy as jnp

    def _L0_xattn_ref(q, k, v, mask, wq, bq, wk, bk, wv, bv, wo, bo):
        import jax, jax.numpy as jnp
        import numpy as np
        import math
        D_MODEL = 128
        N_HEADS = 16
        D_K = D_MODEL // N_HEADS
        B, S = (4, 256)
        b = q.shape[0]

        def split_heads(x):
            return x.reshape(b, -1, N_HEADS, D_K).transpose(0, 2, 1, 3)
        qh = split_heads(q @ wq + bq)
        kh = split_heads(k @ wk + bk)
        vh = split_heads(v @ wv + bv)
        scores = jnp.einsum('bhqd,bhkd->bhqk', qh, kh) / math.sqrt(D_K)
        scores = jnp.where(mask == 0, jnp.float32(-1000000000.0), scores)
        attn = jax.nn.softmax(scores, axis=-1)
        ctx = jnp.einsum('bhqk,bhkd->bhqd', attn, vh)
        ctx = ctx.transpose(0, 2, 1, 3).reshape(b, -1, D_MODEL)
        return ctx @ wo + bo

    def _L0_ffn_ref(x, router_w, router_b, w1, b1, w2, b2):
        import jax, jax.numpy as jnp
        import numpy as np
        DIM = 128
        HIDDEN = 512
        E = 8
        B, S = (2, 512)
        logits = jnp.einsum('bsd,de->bse', x, router_w) + router_b
        probs = jax.nn.softmax(logits, axis=-1)
        top1 = jnp.argmax(probs, axis=-1)
        out = jnp.zeros_like(x)
        for i in range(E):
            h = jnp.einsum('bsd,df->bsf', x, w1[i]) + b1[i]
            a, g = jnp.split(h, 2, axis=-1)
            y = jnp.einsum('bsh,hd->bsd', a * jax.nn.sigmoid(g), w2[i]) + b2[i]
            out = out + jnp.where((top1 == i)[..., None], y, 0.0)
        return out
    x = x + jnp.tanh(g_xattn[0]) * _L0_xattn_ref(_layernorm(x, axis=-1), ctx_1024, ctx_1024, mask_1x1xSxS2_ik0, L0_xattn_wq, L0_xattn_bq, L0_xattn_wk, L0_xattn_bk, L0_xattn_wv, L0_xattn_bv, L0_xattn_wo, L0_xattn_bo)
    x = x + jnp.tanh(g_ffn[0]) * _L0_ffn_ref(_layernorm(x, axis=-1), L0_ffn_router_w, L0_ffn_router_b, L0_ffn_w1, L0_ffn_b1, L0_ffn_w2, L0_ffn_b2)
    return x

_drawn_inputs = setup_inputs


def setup_inputs(seed=0):
    import zlib

    import numpy as np

    out = dict(_drawn_inputs(seed))
    spreads = {'L0_xattn_bq': (0.0, 0.1),
     'L0_xattn_bk': (0.0, 0.8),
     'L0_xattn_bv': (0.0, 0.1),
     'L0_xattn_bo': (0.0, 0.1)}
    factors = {'L0_ffn_b1': 4.347}
    for name, (base, spread) in spreads.items():
        noise = np.random.default_rng([zlib.crc32(name.encode()), seed]).standard_normal(out[name].shape)
        drawn = base * np.exp(spread * noise) if base else spread * noise
        out[name] = jnp.asarray(drawn.astype(out[name].dtype))
    for name, factor in factors.items():
        out[name] = (out[name] * factor).astype(out[name].dtype)
    return out
```

```python
from contextlib import ExitStack

import concourse.bass as bass
from concourse import mybir

ALU = mybir.AluOpType
ACT = mybir.ActivationFunctionType
AX = mybir.AxisListType
F32 = mybir.dt.float32
BF16 = mybir.dt.bfloat16
I32 = mybir.dt.int32

P = 128
MASKED = -(2.0 ** 100)


def need(eng, sem, value):
    if isinstance(value, int) and value <= 0:
        return
    eng.wait_ge(sem, value)


def apart(eng, reached):
    eng.wait_ge(reached, 1)


def gated_xattn_moe(nc, x, ctx_in, mask, g_xattn, g_ffn, wq, bq, wk, bk, wv, bv, wo, bo,
                    router_w, router_b, w1, b1, w2, b2, out):
    B, S, D = x.shape
    C = ctx_in.shape[1]
    H = 16
    DK = D // H
    E = router_w.shape[1]
    F2 = w1.shape[2]
    F = F2 // 2
    FB = F // P
    TB = S // P
    T = B * TB
    N = B * S
    PAIRS = H // 2
    HC = H * C
    HALF = HC // 2
    SCALE = float(DK) ** -0.5
    EPS = 1e-5

    ROW = 2 * D + 8
    REGION = N + P
    FT = T + E - 1
    SPARE = FT - T
    ROWS = E * REGION + SPARE * P
    NO_TOKEN = 2 * N

    routed = nc.dram_tensor("routed_rows", (ROWS, ROW), F32, kind="Internal").ap()
    out_rows = out.rearrange("b s d -> (b s) d")

    with ExitStack() as stack:
        def sb(name, shape, dt=F32):
            return stack.enter_context(nc.sbuf_tensor("sb_" + name, shape, dt))

        def sem(name):
            return stack.enter_context(nc.semaphore(name))

        ident = sb("ident", [P, P])
        identb = sb("identb", [P, P], BF16)
        before = sb("before", [P, P], BF16)
        ones_b = sb("ones_b", [P, P], BF16)
        head_of_row = sb("head_of_row", [P, H])
        v_keep = sb("v_keep", [P, 2, 4])
        head_cols = sb("head_cols", [P, PAIRS, P], BF16)
        rev_expert = sb("rev_expert", [P, E])
        rev_int = sb("rev_int", [P, E], I32)
        region0 = sb("region0", [P, E])
        region_int = sb("region_int", [P, E], I32)
        region_first = sb("region_first", [P, E])
        token_no = sb("token_no", [P, T], I32)
        pad_rows = sb("pad_rows", [P, ROW])
        minus_half = sb("minus_half", [P, T])
        w_q = sb("w_q", [P, D])
        w_k = sb("w_k", [P, D])
        w_v = sb("w_v", [P, D])
        w_o = sb("w_o", [P, D])
        w_r = sb("w_r", [P, E])
        b_q = sb("b_q", [P, 1])
        b_k = sb("b_k", [P, 1])
        b_v = sb("b_v", [P, D])
        b_o = sb("b_o", [P, D])
        b_r = sb("b_r", [P, E])
        gates = sb("gates", [P, 2])
        tanh_g = sb("tanh_g", [P, 2])
        bo_g = sb("bo_g", [P, D])
        w_1 = sb("w_1", [P, E, F2])
        w_2 = sb("w_2", [P, E, FB, D])
        b_2 = sb("b_2", [P, E, D])
        b1_row = sb("b1_row", [E, F2])
        b1_rest = sb("b1_rest", [E, 2, F2])
        b1_part = sb("b1_part", [E, 3, F2], BF16)
        b1_rows = sb("b1_rows", [3, E, F2], BF16)
        xs = sb("xs", [P, T, D])
        ctx_sb = sb("ctx_sb", [P, B // 2, D])
        ctxT = sb("ctxT", [P, B, 2, C])
        kT = sb("kT", [P, B, C])
        v_sb = sb("v_sb", [P, B, D])
        mask_i = sb("mask_i", [P, TB, C], I32)
        mask_b = sb("mask_b", [P, TB, 2, C], BF16)
        seen = sb("seen", [P, TB, C])
        some = sb("some", [P, TB])
        some_b = sb("some_b", [P, TB], BF16)
        q_keep = sb("q_keep", [P, S])
        stats = sb("stats", [P, T, 6])
        mv1 = sb("mv1", [P, T, 2])
        ve1 = sb("ve1", [P, T])
        rstd1 = sb("rstd1", [P, T])
        xh = sb("xh", [P, 2, TB, D])
        turned = sb("turned", [P, 2, 2, S])
        qT = sb("qT", [P, 2, S])
        qm = sb("qm", [P, 2, 2, S], BF16)
        k_bd = sb("k_bd", [P, 2, H, C])
        km = sb("km", [P, 2, 2, HALF], BF16)
        v_st = sb("v_st", [P, 2, 4, 2, 32])
        v_one = sb("v_one", [P, 2, 32])
        top = sb("top", [P, 2, TB, H])
        shift = sb("shift", [P, TB, 2, H], BF16)
        sm = sb("sm", [96, 2, S], BF16)
        pT = sb("pT", [P, 4, 2, S])
        inv = sb("inv", [P, S])
        oT = sb("oT", [P, S])
        xr = sb("xr", [P, 2, TB, ROW])
        st2 = sb("st2", [P, TB, 6])
        mv2 = sb("mv2", [P, 2, TB, 2])
        ve2 = sb("ve2", [P, TB])
        rstd2 = sb("rstd2", [P, TB])
        lg = sb("lg", [P, TB, E])
        lmax = sb("lmax", [P, TB])
        leq = sb("leq", [P, TB, E])
        lrev = sb("lrev", [P, TB, E])
        lbest = sb("lbest", [P, TB])
        onehot = sb("onehot", [P, TB, E], BF16)
        slot = sb("slot", [P, TB, E])
        slot1 = sb("slot1", [P, TB, E])
        pos = sb("pos", [P, 2, TB], I32)
        count = sb("count", [1, E])
        steps_i = sb("steps_i", [1, E, T], I32)
        steps_f = sb("steps_f", [1, E, T])
        over = sb("over", [1, E, T])
        ntile = sb("ntile", [1, E])
        cum = sb("cum", [1, E])
        zero_e = sb("zero_e", [1, E])
        jump = sb("jump", [1, E])
        tile_i = sb("tile_i", [1, FT, E], I32)
        tile_f = sb("tile_f", [1, FT, E])
        past = sb("past", [1, FT, E])
        jumps = sb("jumps", [1, FT, E])
        e_sum = sb("e_sum", [1, FT])
        r_sum = sb("r_sum", [1, FT])
        tile_expert = sb("tile_expert", [1, FT], I32)
        tile_row = sb("tile_row", [1, FT], I32)
        pad_i = sb("pad_i", [P, E], I32)
        part_i = sb("part_i", [P, E], I32)
        part_f = sb("part_f", [P, E])
        NR = 4
        fr = sb("fr", [P, NR, ROW])
        fxT = sb("fxT", [P, 2, P])
        sig = sb("sig", [P, 2, F])
        hid = sb("hid", [P, 2, F])
        hT = sb("hT", [P, 2, F])
        yb = sb("yb", [P, 2, D])
        fo = sb("fo", [P, NR, D])

        def bank(name, n=1):
            return stack.enter_context(nc.psum_tensor("ps_" + name, [P, n * 512], F32))

        psA = bank("A", 2)
        psB = bank("B", 2)
        psO = bank("O")
        psT = bank("T")
        psQ = bank("Q")
        psR = bank("R")
        psR16 = psR[:, :].bitcast(BF16)

        w_in, w_big, x_in, ctx_sem, b1_in, b1_moved = (sem(n) for n in (
            "w_in", "w_big", "x_in", "ctx_in_sem", "b1_in", "b1_moved"))
        const_pool, const_dve = sem("const_pool"), sem("const_dve")
        pads_in = sem("pads_in")
        setup_pe, setup_dve, setup_act = sem("setup_pe"), sem("setup_dve"), sem("setup_act")
        stats_done, rstd_done, ln1_done = sem("stats_done"), sem("rstd_done"), sem("ln1_done")
        tanh_done = sem("tanh_done")
        rstd2_ready, id_ready = sem("rstd2_ready"), sem("id_ready")
        kb_ready, km_ready, vb_ready, qb_ready = sem("kb_ready"), sem("km_ready"), sem("vb_ready"), sem("qb_ready")
        xh_ready, t_psum, t_evac = sem("xh_ready"), sem("t_psum"), sem("t_evac")
        q_psum, q_ready = sem("q_psum"), sem("q_ready")
        a_psum, a_max = sem("a_psum"), sem("a_max")
        shift_hi, shift_ready, shift_psum, sm_ready = (sem(n) for n in (
            "shift_hi", "shift_ready", "shift_psum", "sm_ready"))
        b_psum, p_ready, pv_done = sem("b_psum"), sem("p_ready"), sem("pv_done")
        inv_ready, o_ready = sem("inv_ready"), sem("o_ready")
        wo_psum, x2_ready = sem("wo_psum"), sem("x2_ready")
        st2_done, mv2_ready, xr_ready = sem("st2_done"), sem("mv2_ready"), sem("xr_ready")
        route_psum, route_dve, onehot_ready, rank_psum, pos_ready = (sem(n) for n in (
            "route_psum", "route_dve", "onehot_ready", "rank_psum", "pos_ready"))
        scattered = sem("scattered")
        table_dve, table_pool, table_ready, pad_ready = (sem(n) for n in (
            "table_dve", "table_pool", "table_ready", "pad_ready"))
        padded = sem("padded")
        row_in = [sem(f"row_in{k}") for k in range(NR)]
        stored = [sem(f"stored{k}") for k in range(NR)]
        fo_ready = [sem(f"fo_ready{k}") for k in range(NR)]
        fx_psum, fx_ready, up_psum, sig_ready, hid_ready, ht_psum, ht_ready, y_psum, yb_ready = (
            sem(n) for n in ("fx_psum", "fx_ready", "up_psum", "sig_ready", "hid_ready", "ht_psum",
                             "ht_ready", "y_psum", "yb_ready"))

        W_IN = 12 * 16
        CONSTANTS = 37
        block = stack.enter_context(nc.Block())

        FIRST, LAST = -1, B + 1
        LOOP0, LOOP1 = 4, B - 2

        def steps(eng, step):
            for i in range(FIRST, LOOP0):
                step(i, i % 2)
            with eng.Fori(LOOP0, LOOP1 - 1, 2) as i:
                step(i, 0)
                step(i + 1, 1)
            for i in range(LOOP1, LAST + 1):
                step(i, i % 2)

        def has(b):
            return not isinstance(b, int) or 0 <= b < B

        @block.sync
        def _(sp):
            sp.dma_start(ctx_sb[:, :, :], ctx_in.rearrange("(a b) k d -> (b k) a d", b=2)).then_inc(ctx_sem, 16)
            for dst, src in ((w_k, wk), (w_v, wv), (w_q, wq), (w_o, wo)):
                sp.dma_start(dst[:, :], src).then_inc(w_in, 16)
            sp.dma_start(b_q[:, :], bq.rearrange("(d o) -> d o", o=1)).then_inc(w_in, 16)
            sp.dma_start(b_k[:, :], bk.rearrange("(d o) -> d o", o=1)).then_inc(w_in, 16)
            sp.dma_start(w_r[:, :], router_w).then_inc(w_in, 16)
            xv = x.rearrange("b (t p) d -> p (b t) d", p=P)
            for c in range(4):
                n = T // 4
                sp.dma_start(xs[:, c * n:(c + 1) * n, :], xv[:, c * n:(c + 1) * n, :]).then_inc(x_in, 16)
            sp.dma_start(b1_row[:, :], b1).then_inc(b1_in, 16)
            sp.dma_start(w_1[:, :, :], w1.rearrange("e d f -> d e f")).then_inc(w_big, 16)
            sp.dma_start(w_2[:, :, :, :], w2.rearrange("e (k p) d -> p e k d", p=P)).then_inc(w_big, 16)
            sp.wait_ge(b1_moved, 4)
            for r in range(3):
                sp.dma_start(b1_rows[r:r + 1, :, :], b1_part[:, r, :]).then_inc(w_big, 16)
            sp.wait_ge(const_pool, 2)
            for k in range(SPARE):
                r0 = E * REGION + k * P
                sp.dma_start(routed[r0:r0 + P, :], pad_rows[:, :]).then_inc(pads_in, 16)
            sp.wait_ge(pads_in, 16 * SPARE)
            sp.wait_ge(scattered, 16 * T)
            sp.wait_ge(padded, 16 * E)
            sp.wait_ge(table_ready, 2)

            def fetch(u, k):
                need(sp, stored[k], 16 * u)
                r = sp.value_load(tile_row[0:1, bass.ds(NR * u + k, 1)], min_val=0, max_val=ROWS - P)
                sp.dma_start(fr[:, k, :], routed[bass.ds(r, P), :]).then_inc(row_in[k], 16)
            for k in range(NR):
                fetch(0, k)
            with sp.Fori(1, FT // NR) as u:
                for k in range(NR):
                    fetch(u, k)
            for k in range(FT % NR):
                fetch(FT // NR, k)

        @block.gpsimd
        def _(pool):
            pool.memset(pad_rows[:, :], 0.0).then_inc(const_pool, 1)
            pool.wait_ge(const_pool, 1)
            pool.iota(pad_rows[:, 2 * D:2 * D + 1].bitcast(I32), [[0, 1]], base=NO_TOKEN,
                      channel_multiplier=1).then_inc(const_pool, 1)
            pool.memset(ident[:, :], 0.0).then_inc(const_pool, 1)
            pool.memset(before[:, :], 1.0).then_inc(const_pool, 1)
            pool.memset(ones_b[:, :], 1.0).then_inc(const_pool, 1)
            pool.memset(head_of_row[:, :], 1.0).then_inc(const_pool, 1)
            pool.memset(head_cols[:, :, :], 0.0).then_inc(const_pool, 1)
            pool.memset(km[:, :, :, :], 0.0).then_inc(const_pool, 1)
            pool.memset(v_one[:, :, :], 0.0).then_inc(const_pool, 1)
            pool.memset(v_keep[:, :, :], 0.0).then_inc(const_pool, 1)
            pool.memset(minus_half[:, :], -0.5).then_inc(const_pool, 1)
            pool.memset(zero_e[:, :], 0.0).then_inc(const_pool, 1)
            pool.wait_ge(const_pool, 12)
            pool.affine_select(out=ident[:, :], in_=ident[:, :], compare_op=ALU.not_equal, fill=1.0,
                               base=0, pattern=[[-1, P]], channel_multiplier=1).then_inc(const_pool, 1)
            pool.affine_select(out=before[:, :], in_=before[:, :], compare_op=ALU.is_gt, fill=0.0,
                               base=0, pattern=[[1, P]], channel_multiplier=-1).then_inc(const_pool, 1)
            pool.affine_select(out=head_of_row[:, :], in_=head_of_row[:, :], compare_op=ALU.is_ge, fill=0.0,
                               base=0, pattern=[[-DK, H]], channel_multiplier=1).then_inc(const_pool, 1)
            pool.wait_ge(const_pool, 15)
            pool.affine_select(out=head_of_row[:, :], in_=head_of_row[:, :], compare_op=ALU.is_ge, fill=0.0,
                               base=DK - 1, pattern=[[DK, H]], channel_multiplier=-1).then_inc(const_pool, 1)
            made = [16]

            def alone(ins):
                made[0] += 1
                ins.then_inc(const_pool, 1)
                pool.wait_ge(const_pool, made[0])

            pool.wait_ge(const_pool, made[0])
            alone(pool.affine_select(out=head_cols[0:C, :, :], in_=head_cols[0:C, :, :], compare_op=ALU.not_equal,
                                     fill=1.0, base=0, pattern=[[0, 2 * PAIRS], [-1, C]], channel_multiplier=1))
            for part in range(2):
                alone(pool.affine_select(out=head_cols[C:C + 32, :, :], in_=head_cols[C:C + 32, :, :],
                                         compare_op=ALU.not_equal, fill=1.0, base=-H * part,
                                         pattern=[[-1, H], [0, C]], channel_multiplier=1))
            for par in range(2):
                for hf in range(2):
                    r0 = C * (1 - hf)
                    v = km[r0:r0 + C, par, hf, :]
                    alone(pool.affine_select(out=v, in_=v, compare_op=ALU.not_equal, fill=1.0, base=0,
                                             pattern=[[0, H // 2], [-1, C]], channel_multiplier=1))
            for half in range(2):
                for sub in range(2):
                    hh = 2 * sub + half
                    alone(pool.memset(v_one[C * half:C * half + C, sub, DK * hh:DK * hh + DK], 1.0))
                    alone(pool.memset(v_keep[C * half:C * half + C, sub, hh:hh + 1], 1.0))
            pool.iota(rev_int[:, :], [[-1, E]], base=E, channel_multiplier=0).then_inc(const_pool, 1)
            pool.iota(region_int[:, :], [[REGION, E]], base=0, channel_multiplier=0).then_inc(const_pool, 1)
            pool.iota(token_no[:, :], [[P, T]], base=0, channel_multiplier=1).then_inc(const_pool, 1)
            pool.iota(steps_i[:, :, :], [[0, E], [P, T]], base=0, channel_multiplier=0).then_inc(const_pool, 1)
            pool.iota(tile_i[:, :, :], [[1, FT], [0, E]], base=0, channel_multiplier=0).then_inc(const_pool, 1)
            pool.iota(part_i[:, :], [[0, E]], base=0, channel_multiplier=1).then_inc(const_pool, 1)
            pool.wait_ge(tanh_done, 1)
            pool.wait_ge(w_in, W_IN)
            pool.tensor_scalar(bo_g[:, :], b_o[:, :], tanh_g[:, 0:1], None, ALU.mult).then_inc(ln1_done, 1)
            pool.wait_ge(stats_done, T + 2)
            pool.tensor_tensor(rstd1[:, :], ve1[:, :], minus_half[:, :], ALU.pow).then_inc(rstd_done, 1)
            pool.wait_ge(rstd_done, 1)
            pool.wait_ge(setup_dve, 11)
            pool.wait_ge(const_pool, CONSTANTS)

            def front(b, par):
                need(pool, b_psum, 4 * (b - 1))
                need(pool, km_ready, 2 * (b - 1))
                pool.tensor_tensor(k_bd[:, par, :, :], kT[:, bass.ds(b, 1), :].to_broadcast([P, H, C]),
                                   head_of_row[:, :, None].to_broadcast([P, H, C]), ALU.mult).then_inc(kb_ready, 1)
                need(pool, pv_done, 4 * (b - 1))
                for s in range(2):
                    pool.tensor_tensor(
                        v_st[:, par, :, s, :].rearrange("p g (h d) -> p g h d", d=DK),
                        v_sb[:, bass.ds(b, 1), :].rearrange("p o (g h d) -> p (o g) h d", g=4, d=DK),
                        v_keep[:, s, :][:, None, :, None].to_broadcast([P, 4, 4, DK]),
                        ALU.mult).then_inc(vb_ready, 1)
                pool.wait_ge(xh_ready, 2 * b + 2)
                pool.tensor_tensor(xs[:, bass.ds(b * TB, TB), :], xs[:, bass.ds(b * TB, TB), :],
                                   bo_g[:, None, :].to_broadcast([P, TB, D]), ALU.add).then_inc(ln1_done, 1)

            def step(i, par):
                nxt = 1 - par
                if has(i + 2):
                    front(i + 2, par)
                if has(i - 1):
                    pool.wait_ge(mv2_ready, i)
                    pool.tensor_tensor(rstd2[:, :], ve2[:, :], minus_half[:, 0:TB], ALU.pow).then_inc(rstd2_ready, 1)
                    pool.tensor_copy(xr[:, nxt, :, 2 * D:2 * D + 1].bitcast(I32),
                                     token_no[:, bass.ds((i - 1) * TB, TB)][:, :, None]).then_inc(id_ready, 1)
                if has(i - 2):
                    apart(pool, const_pool)
                    pool.wait_ge(pos_ready, i - 1)
                    pool.wait_ge(xr_ready, 2 * (i - 1))
                    pool.wait_ge(id_ready, i - 1)
                    for t in range(TB):
                        pool.indirect_dma_start(
                            routed[:, :], bass.IndirectOffsetOnAxis(ap=pos[:, par, t:t + 1], axis=0),
                            xr[:, par, t, :], None, bounds_check=ROWS - 1, oob_is_err=True)\
                            .then_inc(scattered, 16)

            front(0, 0)
            steps(pool, step)
            pool.wait_ge(pad_ready, 1)
            for e in range(E):
                pool.indirect_dma_start(
                    routed[:, :], bass.IndirectOffsetOnAxis(ap=pad_i[:, e:e + 1], axis=0),
                    pad_rows[:, :], None, bounds_check=ROWS - 1, oob_is_err=True).then_inc(padded, 16)

            def store(u, k):
                apart(pool, const_pool)
                pool.wait_ge(fo_ready[k], u)
                pool.indirect_dma_start(
                    out_rows, bass.IndirectOffsetOnAxis(ap=fr[:, k, 2 * D:2 * D + 1].bitcast(I32), axis=0),
                    fo[:, k, :], None, bounds_check=N - 1, oob_is_err=False).then_inc(stored[k], 16)
            with pool.Fori(1, FT // NR + 1) as turn:
                for k in range(NR):
                    store(turn, k)
            for t in range(FT // NR * NR, FT):
                store(t // NR + 1, t % NR)
            for k in range(NR):
                pool.wait_ge(stored[k], 16 * ((FT + NR - 1 - k) // NR))

        @block.scalar
        def _(act):
            act.dma_start(gates[:, 0:1], g_xattn.rearrange("(o n) -> o n", o=1).to_broadcast([P, 1])).then_inc(w_in, 16)
            act.dma_start(gates[:, 1:2], g_ffn.rearrange("(o n) -> o n", o=1).to_broadcast([P, 1])).then_inc(w_in, 16)
            act.dma_start(b_v[:, :], bv.rearrange("(o n) -> o n", o=1).to_broadcast([P, D])).then_inc(w_in, 16)
            act.dma_start(b_o[:, :], bo.rearrange("(o n) -> o n", o=1).to_broadcast([P, D])).then_inc(w_in, 16)
            act.dma_start(b_r[:, :], router_b.rearrange("(o n) -> o n", o=1).to_broadcast([P, E])).then_inc(w_in, 16)
            act.dma_start(mask_i[:, :, :], mask.rearrange("a b (t p) c -> p (a b t) c", p=P)).then_inc(ctx_sem, 16)
            act.dma_start(b_2[:, :, :], b2.rearrange("(o e) d -> o e d", o=1).to_broadcast([P, E, D])).then_inc(w_big, 16)
            act.wait_ge(w_in, W_IN)
            act.activation(tanh_g[:, :], gates[:, :], ACT.Tanh).then_inc(tanh_done, 1)

            def keys(b, par):
                act.wait_ge(kb_ready, b + 1)
                need(act, a_psum, 2 * (b - 1))
                for hf in range(2):
                    r0 = C * hf
                    act.activation(km[r0:r0 + C, par, hf, :],
                                   k_bd[r0:r0 + C, par, hf * (H // 2):(hf + 1) * (H // 2), :]
                                   .rearrange("p h c -> p (h c)"), ACT.Copy).then_inc(km_ready, 1)

            def queries(b, par):
                act.wait_ge(q_ready, b + 1)
                need(act, a_psum, 2 * (b - 1))
                for hf in range(2):
                    act.activation(qm[C * hf:C * hf + C, par, hf, :], qT[C * hf:C * hf + C, par, :], ACT.Copy)\
                        .then_inc(qb_ready, 1)

            def exps(i, q0, q1):
                for q in range(q0, q1):
                    act.wait_ge(b_psum, 4 * i + (q + 1))
                    need(act, pv_done, 4 * (i - 1) + (q + 1))
                    act.activation(pT[:, q, :, :].rearrange("p a s -> p (a s)"),
                                   psB[:, (q % 2) * 512:(q % 2 + 1) * 512], ACT.Exp, scale=SCALE).then_inc(p_ready, 1)

            def step(i, par):
                act.wait_ge(t_psum, i + 2)
                if has(i + 1) and has(i - 2):
                    act.activation(turned[:, par, :, :].rearrange("p a s -> p (a s)"), psT[:, :], ACT.Copy)\
                        .then_inc(t_evac, 1)
                else:
                    k = 0 if has(i + 1) else 1
                    if has(i + 1) or has(i - 2):
                        act.activation(turned[:, par, k, :], psT[:, k * S:(k + 1) * S], ACT.Copy).then_inc(t_evac, 1)
                if not has(i):
                    if i == FIRST:
                        queries(0, 0)
                        keys(1, 1)
                    return
                exps(i, 0, 1)
                if has(i + 1):
                    queries(i + 1, 1 - par)
                exps(i, 1, 2)
                if has(i + 2):
                    keys(i + 2, par)
                exps(i, 2, 4)

            keys(0, 0)
            steps(act, step)

            def expert(t, k):
                act.wait_ge(fx_psum, t + 1)
                need(act, up_psum, t - 1)
                act.activation(fxT[:, k, :], psT[:, 0:P], ACT.Copy).then_inc(fx_ready, 1)
                act.wait_ge(up_psum, t + 1)
                need(act, hid_ready, t - 1)
                act.activation(sig[:, k, :], (psA, psB)[k][:, F:F2], ACT.Sigmoid).then_inc(sig_ready, 1)

            def down(t, k):
                act.wait_ge(ht_psum, t + 1)
                need(act, y_psum, t - 1)
                act.activation(hT[:, k, :], psQ[:, :], ACT.Copy).then_inc(ht_ready, 1)

            expert(0, 0)
            for t in range(1, 4):
                expert(t, t % 2)
                down(t - 1, (t - 1) % 2)
            with act.Fori(4, FT - 2, 2) as t:
                expert(t, 0)
                down(t - 1, 1)
                expert(t + 1, 1)
                down(t, 0)
            expert(FT - 1, 0)
            down(FT - 2, 1)
            down(FT - 1, 0)

        @block.vector
        def _(dve):
            dve.wait_ge(const_pool, CONSTANTS)
            dve.tensor_copy(identb[:, :], ident[:, :]).then_inc(const_dve, 1)
            dve.tensor_copy(rev_expert[:, :], rev_int[:, :]).then_inc(const_dve, 1)
            dve.tensor_copy(region0[:, :], region_int[:, :]).then_inc(const_dve, 1)
            dve.tensor_copy(region_first[:, :], region_int[:, :]).then_inc(const_dve, 1)
            dve.tensor_copy(steps_f[:, :, :], steps_i[:, :, :]).then_inc(const_dve, 1)
            dve.tensor_copy(tile_f[:, :, :], tile_i[:, :, :]).then_inc(const_dve, 1)
            dve.tensor_copy(part_f[:, :], part_i[:, :]).then_inc(const_dve, 1)
            dve.memset(xr[:, :, :, 2 * D:], 0.0).then_inc(const_dve, 1)
            dve.wait_ge(ctx_sem, 32)
            dve.tensor_scalar(mask_b[:, :, :, :], mask_i[:, :, None, :].to_broadcast([P, TB, 2, C]), 0.0, MASKED,
                              ALU.is_equal, ALU.mult).then_inc(setup_dve, 1)
            dve.tensor_scalar(seen[:, :, :], mask_i[:, :, :], 0.0, None, ALU.not_equal).then_inc(setup_dve, 1)
            dve.wait_ge(setup_dve, 2)
            dve.tensor_reduce(some[:, :], seen[:, :, :], AX.X, ALU.max).then_inc(setup_dve, 1)
            dve.wait_ge(setup_dve, 3)
            dve.tensor_copy(some_b[:, :], some[:, :]).then_inc(setup_dve, 1)
            for c in range(2):
                dve.wait_ge(setup_pe, c + 1)
                dve.tensor_copy(ctxT[:, 8 * c:8 * c + 8, :, :],
                                (psT, psQ)[c][:, :].rearrange("p (b k) -> p b k", k=C)[:, :, None, :]
                                .to_broadcast([P, 8, 2, C])).then_inc(setup_dve, 1)
            dve.wait_ge(w_in, W_IN)
            dve.wait_ge(setup_pe, 3)
            dve.tensor_scalar(kT[:, :, :].rearrange("p b k -> p (b k)"), psA[:, :], b_k[:, 0:1], None, ALU.add)\
                .then_inc(setup_dve, 1)
            for c in range(4):
                dve.wait_ge(setup_pe, 4 + c)
                dve.tensor_tensor(v_sb[:, 4 * c:4 * c + 4, :], psB[:, (c % 2) * 512:(c % 2 + 1) * 512]
                                  .rearrange("p (b d) -> p b d", d=D), b_v[:, None, :].to_broadcast([P, 4, D]),
                                  ALU.add).then_inc(setup_dve, 1)
            dve.wait_ge(setup_pe, 8)
            for par in range(2):
                dve.tensor_copy(qm[C:P, par, 0, :], psR16[C:P, 0:S]).then_inc(setup_dve, 1)
                dve.tensor_copy(qm[0:C, par, 1, :], psR16[0:C, 0:S]).then_inc(setup_dve, 1)
                dve.tensor_copy(sm[0:C, par, :], psR16[0:C, 0:S]).then_inc(setup_dve, 1)
            dve.tensor_copy(q_keep[:, :], psO[:, 0:S]).then_inc(setup_dve, 1)
            for c in range(4):
                dve.wait_ge(x_in, 64)
                n = T // 4
                with dve.Fori(c * n, (c + 1) * n) as t:
                    dve.bn_stats(stats[:, bass.ds(t, 1), :], xs[:, bass.ds(t, 1), :]).then_inc(stats_done, 1)
                if c == 0:
                    pass
            dve.wait_ge(stats_done, T)
            for t in range(T):
                last = dve.bn_aggr(mv1[:, t, :], stats[:, t, :])
            last.then_inc(stats_done, 1)
            dve.wait_ge(stats_done, T + 1)
            dve.tensor_scalar(ve1[:, :], mv1[:, :, 1], EPS, None, ALU.add).then_inc(stats_done, 1)
            dve.wait_ge(b1_in, 16)
            dve.tensor_copy(b1_part[:, 0, :], b1_row[:, :]).then_inc(b1_moved, 1)
            dve.wait_ge(b1_moved, 1)
            dve.tensor_tensor(b1_rest[:, 0, :], b1_row[:, :], b1_part[:, 0, :], ALU.subtract).then_inc(b1_moved, 1)
            dve.wait_ge(b1_moved, 2)
            dve.tensor_copy(b1_part[:, 1, :], b1_rest[:, 0, :]).then_inc(b1_moved, 1)
            dve.wait_ge(b1_moved, 3)
            dve.tensor_tensor(b1_part[:, 2, :], b1_rest[:, 0, :], b1_part[:, 1, :], ALU.subtract).then_inc(b1_moved, 1)
            dve.wait_ge(rstd_done, 1)

            def normalize(b, par):
                need(dve, t_psum, b - 1)
                for t in range(TB):
                    dve.tensor_scalar(xh[:, par, t, :], xs[:, bass.ds(b * TB + t, 1), :],
                                      mv1[:, bass.ds(b * TB + t, 1), 0:1], rstd1[:, bass.ds(b * TB + t, 1)],
                                      ALU.subtract, ALU.mult).then_inc(xh_ready, 1)

            normalize(0, 0)

            def step(i, par):
                nxt = 1 - par
                if has(i + 2) and not has(i - 1):
                    normalize(i + 2, par)
                if has(i + 1):
                    dve.wait_ge(q_psum, i + 2)
                    need(dve, b_psum, 4 * i)
                    need(dve, qb_ready, 2 * i)
                    dve.scalar_tensor_tensor(out=qT[:, nxt, :], in0=psQ[:, 0:S], scalar=b_q[:, 0:1],
                                             in1=q_keep[:, :], op0=ALU.add, op1=ALU.mult).then_inc(q_ready, 1)
                if has(i - 1):
                    dve.wait_ge(wo_psum, i)
                    dve.wait_ge(ln1_done, i + 1)
                    need(dve, scattered, 32 * (i - 2))
                    dve.scalar_tensor_tensor(out=xr[:, nxt, :, 0:D], in0=psQ[:, S:2 * S].rearrange("p (t d) -> p t d", d=D),
                                             scalar=tanh_g[:, 0:1], in1=xs[:, bass.ds((i - 1) * TB, TB), :],
                                             op0=ALU.mult, op1=ALU.add).then_inc(x2_ready, 1)
                if has(i + 1):
                    dve.wait_ge(a_psum, 2 * (i + 1) + 1)
                    dve.tensor_reduce(top[:, nxt, 0, :], psA[:, :].rearrange("p (h k) -> p h k", k=C), AX.X,
                                      ALU.max).then_inc(a_max, 1)
                if has(i - 1):
                    dve.wait_ge(x2_ready, i)
                    for t in range(TB):
                        dve.bn_stats(st2[:, t, :], xr[:, nxt, t, 0:D]).then_inc(st2_done, 1)
                    need(dve, rstd2_ready, i - 1)
                    dve.wait_ge(st2_done, 4 * (i - 1) + 2)
                    if has(i + 2):
                        normalize(i + 2, par)
                    for t in range(TB):
                        dve.bn_aggr(mv2[:, nxt, t, :], st2[:, t, :]).then_inc(st2_done, 1)
                    dve.wait_ge(st2_done, 4 * (i - 1) + 4)
                    dve.tensor_scalar(ve2[:, :], mv2[:, nxt, :, 1], EPS, None, ALU.add).then_inc(mv2_ready, 1)
                if has(i - 2):
                    dve.wait_ge(route_psum, i - 1)
                    dve.tensor_tensor(lg[:, :, :], psR[:, 0:TB * E].rearrange("p (t e) -> p t e", e=E),
                                      b_r[:, None, :].to_broadcast([P, TB, E]), ALU.add).then_inc(route_dve, 1)
                    dve.wait_ge(route_dve, 7 * (i - 2) + 1)
                    dve.tensor_reduce(lmax[:, :], lg[:, :, :], AX.X, ALU.max).then_inc(route_dve, 1)
                    dve.wait_ge(route_dve, 7 * (i - 2) + 2)
                    dve.tensor_tensor(leq[:, :, :], lg[:, :, :], lmax[:, :, None].to_broadcast([P, TB, E]),
                                      ALU.is_equal).then_inc(route_dve, 1)
                    dve.wait_ge(route_dve, 7 * (i - 2) + 3)
                    dve.tensor_tensor(lrev[:, :, :], leq[:, :, :], rev_expert[:, None, :].to_broadcast([P, TB, E]),
                                      ALU.mult).then_inc(route_dve, 1)
                    dve.wait_ge(route_dve, 7 * (i - 2) + 4)
                    dve.tensor_reduce(lbest[:, :], lrev[:, :, :], AX.X, ALU.max).then_inc(route_dve, 1)
                    dve.wait_ge(route_dve, 7 * (i - 2) + 5)
                    dve.tensor_tensor(onehot[:, :, :], lrev[:, :, :], lbest[:, :, None].to_broadcast([P, TB, E]),
                                      ALU.is_equal).then_inc(onehot_ready, 1)
                if has(i + 1):
                    dve.wait_ge(a_psum, 2 * (i + 1) + 2)
                    dve.tensor_reduce(top[:, nxt, 1, :], psA[:, :].rearrange("p (h k) -> p h k", k=C), AX.X,
                                      ALU.max).then_inc(a_max, 1)
                    dve.wait_ge(a_max, 2 * (i + 1) + 2)
                    need(dve, shift_psum, i + 1)
                    dve.tensor_scalar(shift[:, :, 0, :], top[:, nxt, :, :], -1.0, None, ALU.mult).then_inc(shift_hi, 1)
                    dve.wait_ge(shift_hi, i + 2)
                    dve.scalar_tensor_tensor(out=shift[:, :, 1, :], in0=top[:, nxt, :, :], scalar=-1.0,
                                             in1=shift[:, :, 0, :], op0=ALU.mult, op1=ALU.subtract)\
                        .then_inc(shift_ready, 1)
                if has(i - 1):
                    dve.wait_ge(rstd2_ready, i)
                    for t in range(TB):
                        dve.tensor_scalar(xr[:, nxt, t, D:2 * D], xr[:, nxt, t, 0:D], mv2[:, nxt, t, 0:1],
                                          rstd2[:, t:t + 1], ALU.subtract, ALU.mult).then_inc(xr_ready, 1)
                if has(i - 2):
                    dve.wait_ge(rank_psum, i - 1)
                    dve.tensor_tensor(slot[:, :, :], psR[:, 32:32 + TB * E].rearrange("p (t e) -> p t e", e=E),
                                      region0[:, None, :].to_broadcast([P, TB, E]), ALU.add).then_inc(route_dve, 1)
                    dve.wait_ge(route_dve, 7 * (i - 2) + 6)
                    dve.tensor_tensor(slot1[:, :, :], slot[:, :, :], onehot[:, :, :], ALU.mult).then_inc(route_dve, 1)
                    dve.tensor_tensor(region0[:, :], psR[:, 64:64 + E], region0[:, :], ALU.add)
                    dve.wait_ge(route_dve, 7 * (i - 2) + 7)
                    need(dve, scattered, 32 * (i - 3))
                    with nc.allow_low_precision(reason="row numbers: integers below 2**24"):
                        dve.tensor_reduce(pos[:, par, :], slot1[:, :, :], AX.X, ALU.add).then_inc(pos_ready, 1)
                if has(i + 1):
                    dve.wait_ge(shift_psum, i + 2)
                    need(dve, b_psum, 4 * i)
                    dve.tensor_copy(sm[C:C + 32, nxt, :], psR16[0:32, 512:512 + S]).then_inc(sm_ready, 1)
                if has(i):
                    dve.wait_ge(pv_done, 4 * i + 4)
                    need(dve, o_ready, i)
                    dve.reciprocal(inv[:, :], psO[:, S:2 * S]).then_inc(inv_ready, 1)
                    dve.wait_ge(inv_ready, i + 1)
                    need(dve, wo_psum, i)
                    dve.tensor_tensor(oT[:, :], psO[:, 0:S], inv[:, :], ALU.mult).then_inc(o_ready, 1)

            steps(dve, step)

            dve.wait_ge(pos_ready, B)
            chain = [0]

            def link(ins):
                chain[0] += 1
                ins.then_inc(table_dve, 1)
                dve.wait_ge(table_dve, chain[0])
            dve.tensor_tensor(pad_i[:, :], part_f[:, :], region0[:, :], ALU.add).then_inc(pad_ready, 1)
            link(dve.tensor_tensor(count[:, :], region0[0:1, :], region_first[0:1, :], ALU.subtract))
            link(dve.tensor_tensor(over[:, :, :], count[:, :, None].to_broadcast([1, E, T]), steps_f[:, :, :], ALU.is_gt))
            link(dve.tensor_reduce(ntile[:, :], over[:, :, :], AX.X, ALU.add))
            link(dve.tensor_tensor_scan(cum[:, :], ntile[:, :], zero_e[:, :], 0.0, ALU.add, ALU.add))
            link(dve.tensor_scalar(jump[:, :], ntile[:, :], -float(P), float(REGION), ALU.mult, ALU.add))
            link(dve.tensor_tensor(past[:, :, :], tile_f[:, :, :], cum[:, None, :].to_broadcast([1, FT, E]), ALU.is_ge))
            link(dve.tensor_tensor(jumps[:, :, :], past[:, :, :], jump[:, None, :].to_broadcast([1, FT, E]), ALU.mult))
            link(dve.tensor_reduce(e_sum[:, :], past[:, :, :], AX.X, ALU.add))
            link(dve.tensor_reduce(r_sum[:, :], jumps[:, :, :], AX.X, ALU.add))
            dve.tensor_scalar(tile_expert[:, :], e_sum[:, :], float(E - 1), None, ALU.min).then_inc(table_ready, 1)
            dve.scalar_tensor_tensor(out=tile_row[:, :], in0=tile_f[:, :, 0], scalar=float(P), in1=r_sum[:, :],
                                     op0=ALU.mult, op1=ALU.add).then_inc(table_ready, 1)

            dve.wait_ge(table_ready, 2)

            def gate(t, k):
                dve.wait_ge(sig_ready, t + 1)
                need(dve, ht_psum, t - 1)
                dve.tensor_tensor(hid[:, k, :], (psA, psB)[k][:, 0:F], sig[:, k, :], ALU.mult).then_inc(hid_ready, 1)

            def finish(u, k):
                t = NR * u + k
                e = dve.value_load(tile_expert[0:1, bass.ds(t, 1)], min_val=0, max_val=E - 1)
                dve.wait_ge(y_psum, t + 1)
                dve.tensor_tensor(yb[:, k % 2, :], psO[:, 0:D], b_2[:, bass.ds(e, 1), :].rearrange("p o d -> p (o d)"),
                                  ALU.add).then_inc(yb_ready, 1)
                dve.wait_ge(yb_ready, t + 1)
                need(dve, stored[k], 16 * u)
                dve.scalar_tensor_tensor(out=fo[:, k, :], in0=yb[:, k % 2, :], scalar=tanh_g[:, 1:2],
                                         in1=fr[:, k, 0:D], op0=ALU.mult, op1=ALU.add).then_inc(fo_ready[k], 1)

            gate(0, 0)
            dve.wait_ge(w_big, 96)
            for k in range(NR):
                gate(k + 1, (k + 1) % 2)
                finish(0, k)
            with dve.Fori(1, FT // NR) as u:
                for k in range(NR):
                    gate(NR * u + (k + 1), (k + 1) % 2)
                    finish(u, k)
            for t in range(FT // NR * NR, FT):
                if t + 1 < FT:
                    gate(t + 1, (t + 1) % 2)
                finish(t // NR, t % NR)

        @block.tensor
        def _(pe):
            pe.wait_ge(const_pool, CONSTANTS)
            pe.wait_ge(ctx_sem, 32)
            for c in range(2):
                for k in range(4):
                    last = pe.transpose((psT, psQ)[c][:, k * P:(k + 1) * P], ctx_sb[:, 4 * c + k, :], ident[:, :])
                last.then_inc(setup_pe, 1)
            pe.wait_ge(w_in, W_IN)
            for c in range(2):
                pe.wait_ge(setup_dve, 5 + c)
                last = pe.matmul(psA[:, c * 512:(c + 1) * 512], w_k[:, :], ctxT[:, 8 * c:8 * c + 8, 0, :],
                                 start=True, stop=True)
            last.then_inc(setup_pe, 1)
            for c in range(4):
                if c >= 2:
                    pe.wait_ge(setup_dve, 8 + c - 2)
                for k in range(4):
                    b = 4 * c + k
                    col = (c % 2) * 512 + k * D
                    last = pe.matmul(psB[:, col:col + D], ctxT[:, b, :, :].rearrange("p a k -> p (a k)"), w_v[:, :],
                                     start=True, stop=True)
                last.then_inc(setup_pe, 1)
            pe.wait_ge(setup_dve, 4)
            pe.wait_ge(const_dve, 1)
            for t in range(TB):
                pe.transpose(psR16[:, t * P:(t + 1) * P], mask_b[:, t, :, :].rearrange("p a k -> p (a k)"), identb[:, :])
            for t in range(TB):
                last = pe.matmul(psO[:, t * P:(t + 1) * P], some_b[:, t:t + 1].to_broadcast([P, P]), identb[:, :],
                                 start=True, stop=True)
            last.then_inc(setup_pe, 1)

            def step(i, par):
                nxt = 1 - par

                def scores(q):
                    need(pe, p_ready, 4 * i + (q + 1) - 2)
                    for k in range(2):
                        p = 2 * q + k
                        o = psB[:, (q % 2) * 512 + k * S:(q % 2) * 512 + (k + 1) * S]
                        pe.matmul(o, k_bd[:, par, 2 * p:2 * p + 2, :].rearrange("p h k -> p (h k)"), qT[:, par, :],
                                  start=True, stop=False)
                        last = pe.matmul(o, head_cols[0:C + 32, p, :], sm[:, par, :], start=False, stop=True)
                    last.then_inc(b_psum, 1)

                def values(q):
                    pe.wait_ge(p_ready, 4 * i + (q + 1))
                    if q == 0:
                        need(pe, o_ready, i)
                        pe.wait_ge(vb_ready, 2 * i + 2)
                    rows = slice(32 * q, 32 * q + 32)
                    for k in range(2):
                        pe.matmul(psO[rows, 0:S], v_st[:, par, q, k, :], pT[:, q, k, :], start=(k == 0), stop=(k == 1),
                                  tile_position=(0, 32 * q))
                    for k in range(2):
                        last = pe.matmul(psO[rows, S:2 * S], v_one[:, k, :], pT[:, q, k, :], start=(k == 0),
                                         stop=(k == 1), tile_position=(0, 32 * q))
                    last.then_inc(pv_done, 1)

                def maxima(t):
                    need(pe, a_max, 2 * (i + 1) + t)
                    for hf in range(2):
                        last = pe.matmul(psA[:, hf * HALF:(hf + 1) * HALF], qm[:, nxt, hf, t * P:(t + 1) * P],
                                         km[:, nxt, hf, :], start=True, stop=True)
                    last.then_inc(a_psum, 1)

                need(pe, t_evac, i + 1)
                last = None
                if has(i + 1):
                    pe.wait_ge(xh_ready, 2 * (i + 2))
                    for t in range(TB):
                        last = pe.transpose(psT[:, t * P:(t + 1) * P], xh[:, nxt, t, :], ident[:, :])
                if has(i - 2):
                    pe.wait_ge(xr_ready, 2 * (i - 1))
                    for t in range(TB):
                        last = pe.transpose(psT[:, S + t * P:S + (t + 1) * P], xr[:, par, t, D:2 * D], ident[:, :])
                last.then_inc(t_psum, 1)
                if has(i):
                    pe.wait_ge(sm_ready, i + 1)
                    pe.wait_ge(kb_ready, i + 1)
                    scores(0)
                if has(i + 1):
                    pe.wait_ge(t_evac, i + 2)
                    need(pe, x2_ready, i - 1)
                    pe.matmul(psQ[:, 0:S], w_q[:, :], turned[:, par, 0, :], start=True, stop=True).then_inc(q_psum, 1)
                if has(i):
                    scores(1)
                if has(i - 2):
                    pe.wait_ge(t_evac, i + 2)
                    need(pe, sm_ready, min(i + 1, B) if isinstance(i, int) else i + 1)
                    need(pe, pos_ready, i - 2)
                    for t in range(TB):
                        last = pe.matmul(psR[:, t * E:(t + 1) * E], turned[:, par, 1, t * P:(t + 1) * P], w_r[:, :],
                                         start=True, stop=True)
                    last.then_inc(route_psum, 1)
                if has(i):
                    values(0)
                if has(i - 1):
                    pe.wait_ge(o_ready, i)
                    need(pe, q_ready, min(i + 2, B) if isinstance(i, int) else i + 2)
                    for t in range(TB):
                        last = pe.matmul(psQ[:, S + t * D:S + (t + 1) * D], oT[:, t * P:(t + 1) * P], w_o[:, :],
                                         start=True, stop=True)
                    last.then_inc(wo_psum, 1)
                if has(i + 1):
                    pe.wait_ge(qb_ready, 2 * (i + 2))
                    pe.wait_ge(km_ready, 2 * (i + 2))
                    maxima(0)
                if has(i):
                    scores(2)
                    values(1)
                if has(i + 1):
                    maxima(1)
                if has(i - 2):
                    pe.wait_ge(onehot_ready, i - 1)
                    for t in range(TB):
                        pe.matmul(psR[:, 32 + t * E:32 + (t + 1) * E], before[:, :], onehot[:, t, :], start=(t == 0),
                                  stop=False, skip_group_check=True)
                    pe.matmul(psR[:, 32 + E:32 + 2 * E], ones_b[:, :], onehot[:, 0, :], start=False, stop=True,
                              skip_group_check=True)
                    for t in range(TB):
                        last = pe.matmul(psR[:, 64:64 + E], ones_b[:, :], onehot[:, t, :], start=False,
                                         stop=(t == TB - 1), skip_group_check=True)
                    last.then_inc(rank_psum, 1)
                if has(i):
                    scores(3)
                    values(2)
                    values(3)
                if has(i + 1):
                    pe.wait_ge(shift_ready, i + 2)
                    need(pe, pos_ready, i - 1)
                    for t in range(TB):
                        last = pe.transpose(psR16[0:32, 512 + t * P:512 + (t + 1) * P],
                                            shift[:, t, :, :].rearrange("p a h -> p (a h)"), identb[:, :])
                    last.then_inc(shift_psum, 1)

            pe.wait_ge(setup_dve, 18)
            steps(pe, step)

            pe.wait_ge(table_ready, 2)
            pe.wait_ge(w_big, 96)

            def turn(t, k, k4):
                pe.wait_ge(row_in[k4], 4 * (t - k4) + 16)
                need(pe, fx_ready, t)
                pe.transpose(psT[:, 0:P], fr[:, k4, D:2 * D], ident[:, :]).then_inc(fx_psum, 1)

            def up(t, k):
                ps = (psA, psB)[k]
                e = pe.value_load(tile_expert[0:1, bass.ds(t, 1)], min_val=0, max_val=E - 1)
                pe.wait_ge(fx_ready, t + 1)
                need(pe, hid_ready, t - 1)
                for c in (1, 0):
                    o = ps[:, c * F:(c + 1) * F]
                    pe.matmul(o, ones_b[0:3, :], b1_rows[:, bass.ds(e, 1), c * F:(c + 1) * F], start=True, stop=False)
                    last = pe.matmul(o, fxT[:, k, :], w_1[:, bass.ds(e, 1), c * F:(c + 1) * F], start=False, stop=True)
                last.then_inc(up_psum, 1)

            def down(t, k):
                e = pe.value_load(tile_expert[0:1, bass.ds(t, 1)], min_val=0, max_val=E - 1)
                pe.wait_ge(hid_ready, t + 1)
                need(pe, ht_ready, t)
                for f in range(FB):
                    last = pe.transpose(psQ[:, f * P:(f + 1) * P], hid[:, k, f * P:(f + 1) * P], ident[:, :])
                last.then_inc(ht_psum, 1)
                return e

            def down2(t, k, e):
                pe.wait_ge(ht_ready, t + 1)
                need(pe, yb_ready, t)
                for f in range(FB):
                    last = pe.matmul(psO[:, 0:D], hT[:, k, f * P:(f + 1) * P],
                                     w_2[:, bass.ds(e, 1), f:f + 1, :], start=(f == 0), stop=(f == FB - 1))
                last.then_inc(y_psum, 1)

            turn(0, 0, 0)
            up(0, 0)
            turn(1, 1, 1)

            def tile(t, k, k4):
                up(t + 1, 1 - k)
                e = down(t, k)
                turn(t + 2, k, (k4 + 2) % 4)
                down2(t, k, e)

            for t in range(4):
                tile(t, t % 2, t)
            with pe.Fori(NR, FT - 6, NR) as t:
                for k in range(4):
                    tile(t + k, k % 2, k)
            for t in range(FT - 3, FT):
                if t + 1 < FT:
                    up(t + 1, (t + 1) % 2)
                e = down(t, t % 2)
                if t + 2 < FT:
                    turn(t + 2, t % 2, (t + 2) % 4)
                down2(t, t % 2, e)


_INS = ['x', 'ctx_1024', 'mask_1x1xSxS2_ik0', 'g_xattn', 'g_ffn', 'L0_xattn_wq', 'L0_xattn_bq', 'L0_xattn_wk',
        'L0_xattn_bk', 'L0_xattn_wv', 'L0_xattn_bv', 'L0_xattn_wo', 'L0_xattn_bo', 'L0_ffn_router_w',
        'L0_ffn_router_b', 'L0_ffn_w1', 'L0_ffn_b1', 'L0_ffn_w2', 'L0_ffn_b2']


def kernel(**inputs):
    import numpy as _np
    import concourse.bacc as _bacc
    from concourse import mybir as _mybir
    from concourse.bass_utils import run_bass_kernel_spmd as _run

    nc = _bacc.Bacc("TRN2", target_bir_lowering=False, num_devices=1)
    arrays, args = {}, []
    for name in _INS:
        a = _np.ascontiguousarray(inputs[name])
        arrays[f"in_{name}_dram"] = a
        args.append(nc.dram_tensor(f"in_{name}_dram", a.shape, _mybir.dt.from_np(a.dtype), kind="ExternalInput").ap())
    shape = inputs['x'].shape
    out = nc.dram_tensor("out_0_dram", shape, _mybir.dt.float32, kind="ExternalOutput").ap()
    gated_xattn_moe(nc, *args, out)
    r = _run(nc, [arrays], core_ids=[0])
    return r.results[0]["out_0_dram"]
```

```python
from contextlib import ExitStack

import concourse.bass as bass
from concourse import mybir

ALU = mybir.AluOpType
ACT = mybir.ActivationFunctionType
AX = mybir.AxisListType
F32 = mybir.dt.float32
BF16 = mybir.dt.bfloat16
I32 = mybir.dt.int32

P = 128
MASKED = -(2.0 ** 100)


def need(eng, sem, value):
    if isinstance(value, int) and value <= 0:
        return
    eng.wait_ge(sem, value)


def apart(eng, reached):
    eng.wait_ge(reached, 1)


def gated_xattn_moe(nc, x, ctx_in, mask, g_xattn, g_ffn, wq, bq, wk, bk, wv, bv, wo, bo,
                    router_w, router_b, w1, b1, w2, b2, out):
    B, S, D = x.shape
    C = ctx_in.shape[1]
    H = 16
    DK = D // H
    E = router_w.shape[1]
    F2 = w1.shape[2]
    F = F2 // 2
    FB = F // P
    TB = S // P
    T = B * TB
    N = B * S
    PAIRS = H // 2
    HC = H * C
    HALF = HC // 2
    SCALE = float(DK) ** -0.5
    EPS = 1e-5

    ROW = 2 * D + 8
    REGION = N + P
    FT = T + E - 1
    SPARE = FT - T
    ROWS = E * REGION + SPARE * P
    NO_TOKEN = 2 * N

    routed = nc.dram_tensor("routed_rows", (ROWS, ROW), F32, kind="Internal").ap()
    out_rows = out.rearrange("b s d -> (b s) d")

    with ExitStack() as stack:
        def sb(name, shape, dt=F32):
            return stack.enter_context(nc.sbuf_tensor("sb_" + name, shape, dt))

        def sem(name):
            return stack.enter_context(nc.semaphore(name))

        ident = sb("ident", [P, P])
        identb = sb("identb", [P, P], BF16)
        before = sb("before", [P, P], BF16)
        ones_b = sb("ones_b", [P, P], BF16)
        head_of_row = sb("head_of_row", [P, H])
        v_keep = sb("v_keep", [P, 2, 4])
        head_cols = sb("head_cols", [P, PAIRS, P], BF16)
        rev_expert = sb("rev_expert", [P, E])
        rev_int = sb("rev_int", [P, E], I32)
        region0 = sb("region0", [P, E])
        region_int = sb("region_int", [P, E], I32)
        region_first = sb("region_first", [P, E])
        token_no = sb("token_no", [P, T], I32)
        pad_rows = sb("pad_rows", [P, ROW])
        minus_half = sb("minus_half", [P, T])
        w_q = sb("w_q", [P, D])
        w_k = sb("w_k", [P, D])
        w_v = sb("w_v", [P, D])
        w_o = sb("w_o", [P, D])
        w_r = sb("w_r", [P, E])
        b_q = sb("b_q", [P, 1])
        b_k = sb("b_k", [P, 1])
        b_v = sb("b_v", [P, D])
        b_o = sb("b_o", [P, D])
        b_r = sb("b_r", [P, E])
        gates = sb("gates", [P, 2])
        tanh_g = sb("tanh_g", [P, 2])
        bo_g = sb("bo_g", [P, D])
        w_1 = sb("w_1", [P, E, F2])
        w_2 = sb("w_2", [P, E, FB, D])
        b_2 = sb("b_2", [P, E, D])
        b1_row = sb("b1_row", [E, F2])
        b1_rest = sb("b1_rest", [E, 2, F2])
        b1_part = sb("b1_part", [E, 3, F2], BF16)
        b1_rows = sb("b1_rows", [3, E, F2], BF16)
        xs = sb("xs", [P, T, D])
        ctx_sb = sb("ctx_sb", [P, B // 2, D])
        ctxT = sb("ctxT", [P, B, 2, C])
        kT = sb("kT", [P, B, C])
        v_sb = sb("v_sb", [P, B, D])
        mask_i = sb("mask_i", [P, TB, C], I32)
        mask_b = sb("mask_b", [P, TB, 2, C], BF16)
        seen = sb("seen", [P, TB, C])
        some = sb("some", [P, TB])
        some_b = sb("some_b", [P, TB], BF16)
        q_keep = sb("q_keep", [P, S])
        stats = sb("stats", [P, T, 6])
        mv1 = sb("mv1", [P, T, 2])
        ve1 = sb("ve1", [P, T])
        rstd1 = sb("rstd1", [P, T])
        xh = sb("xh", [P, 2, TB, D])
        turned = sb("turned", [P, 2, 2, S])
        qT = sb("qT", [P, 2, S])
        qm = sb("qm", [P, 2, 2, S], BF16)
        k_bd = sb("k_bd", [P, 2, H, C])
        km = sb("km", [P, 2, 2, HALF], BF16)
        v_st = sb("v_st", [P, 2, 4, 2, 32])
        v_one = sb("v_one", [P, 2, 32])
        top = sb("top", [P, 2, TB, H])
        shift = sb("shift", [P, TB, 2, H], BF16)
        sm = sb("sm", [96, 2, S], BF16)
        pT = sb("pT", [P, 4, 2, S])
        inv = sb("inv", [P, S])
        oT = sb("oT", [P, S])
        xr = sb("xr", [P, 2, TB, ROW])
        st2 = sb("st2", [P, TB, 6])
        mv2 = sb("mv2", [P, 2, TB, 2])
        ve2 = sb("ve2", [P, TB])
        rstd2 = sb("rstd2", [P, TB])
        hold = sb("hold", [1, 1])
        lg = sb("lg", [P, TB, E])
        lmax = sb("lmax", [P, TB])
        leq = sb("leq", [P, TB, E])
        lrev = sb("lrev", [P, TB, E])
        lbest = sb("lbest", [P, TB])
        onehot = sb("onehot", [P, TB, E], BF16)
        slot = sb("slot", [P, TB, E])
        slot1 = sb("slot1", [P, TB, E])
        pos = sb("pos", [P, 2, TB], I32)
        count = sb("count", [1, E])
        steps_i = sb("steps_i", [1, E, T], I32)
        steps_f = sb("steps_f", [1, E, T])
        over = sb("over", [1, E, T])
        ntile = sb("ntile", [1, E])
        cum = sb("cum", [1, E])
        zero_e = sb("zero_e", [1, E])
        jump = sb("jump", [1, E])
        tile_i = sb("tile_i", [1, FT, E], I32)
        tile_f = sb("tile_f", [1, FT, E])
        past = sb("past", [1, FT, E])
        jumps = sb("jumps", [1, FT, E])
        e_sum = sb("e_sum", [1, FT])
        r_sum = sb("r_sum", [1, FT])
        tile_expert = sb("tile_expert", [1, FT], I32)
        tile_row = sb("tile_row", [1, FT], I32)
        pad_i = sb("pad_i", [P, E], I32)
        part_i = sb("part_i", [P, E], I32)
        part_f = sb("part_f", [P, E])
        NR = 6
        fr = sb("fr", [P, NR, ROW])
        fxT = sb("fxT", [P, 2, P])
        pT_flat = pT[:, :, :, :].rearrange("p q a s -> p q (a s)")
        sig, hid = pT_flat[:, 0:2, :], pT_flat[:, 2:4, :]
        hT = k_bd[:, :, :, :].rearrange("p a h c -> p a (h c)")[:, :, 0:F]
        yb = sb("yb", [P, 2, D])
        fo = sb("fo", [P, NR, D])

        def bank(name, n=1):
            return stack.enter_context(nc.psum_tensor("ps_" + name, [P, n * 512], F32))

        psA = bank("A", 2)
        psB = bank("B", 2)
        psO = bank("O")
        psT = bank("T")
        psQ = bank("Q")
        psR = bank("R")
        psR16 = psR[:, :].bitcast(BF16)

        w_in, w_big, x_in, ctx_sem, b1_in, b1_moved = (sem(n) for n in (
            "w_in", "w_big", "x_in", "ctx_in_sem", "b1_in", "b1_moved"))
        const_pool, const_dve = sem("const_pool"), sem("const_dve")
        pads_in = sem("pads_in")
        setup_pe, setup_dve, setup_act = sem("setup_pe"), sem("setup_dve"), sem("setup_act")
        stats_done, rstd_done, ln1_done = sem("stats_done"), sem("rstd_done"), sem("ln1_done")
        tanh_done = sem("tanh_done")
        rstd2_ready, id_ready = sem("rstd2_ready"), sem("id_ready")
        kb_ready, km_ready, vb_ready, qb_ready = sem("kb_ready"), sem("km_ready"), sem("vb_ready"), sem("qb_ready")
        xh_ready, t_psum, t_evac = sem("xh_ready"), sem("t_psum"), sem("t_evac")
        q_psum, q_ready = sem("q_psum"), sem("q_ready")
        a_psum, a_max = sem("a_psum"), sem("a_max")
        shift_hi, shift_ready, shift_psum, sm_ready = (sem(n) for n in (
            "shift_hi", "shift_ready", "shift_psum", "sm_ready"))
        b_psum, p_ready, pv_done = sem("b_psum"), sem("p_ready"), sem("pv_done")
        inv_ready, o_ready = sem("inv_ready"), sem("o_ready")
        wo_psum, x2_ready = sem("wo_psum"), sem("x2_ready")
        st2_done, mv2_ready, xr_ready = sem("st2_done"), sem("mv2_ready"), sem("xr_ready")
        route_psum, route_dve, onehot_ready, rank_psum, pos_ready = (sem(n) for n in (
            "route_psum", "route_dve", "onehot_ready", "rank_psum", "pos_ready"))
        scattered = sem("scattered")
        table_dve, table_pool, table_ready, pad_ready = (sem(n) for n in (
            "table_dve", "table_pool", "table_ready", "pad_ready"))
        padded = sem("padded")
        row_in = [sem(f"row_in{k}") for k in range(NR)]
        stored = [sem(f"stored{k}") for k in range(NR)]
        fo_ready = [sem(f"fo_ready{k}") for k in range(NR)]
        fx_psum, fx_ready, up_psum, sig_ready, hid_ready, ht_psum, ht_ready, y_psum, yb_ready = (
            sem(n) for n in ("fx_psum", "fx_ready", "up_psum", "sig_ready", "hid_ready", "ht_psum",
                             "ht_ready", "y_psum", "yb_ready"))

        W_IN = 12 * 16
        CONSTANTS = 37
        block = stack.enter_context(nc.Block())

        FIRST, LAST = -1, B + 1
        LOOP0, LOOP1 = 4, B - 2

        def steps(eng, step):
            for i in range(FIRST, LOOP0):
                step(i, i % 2)
            with eng.Fori(LOOP0, LOOP1 - 1, 2) as i:
                step(i, 0)
                step(i + 1, 1)
            for i in range(LOOP1, LAST + 1):
                step(i, i % 2)

        def has(b):
            return not isinstance(b, int) or 0 <= b < B

        @block.sync
        def _(sp):
            sp.dma_start(ctx_sb[:, :, :], ctx_in.rearrange("(a b) k d -> (b k) a d", b=2)).then_inc(ctx_sem, 16)
            for dst, src in ((w_k, wk), (w_v, wv), (w_q, wq), (w_o, wo)):
                sp.dma_start(dst[:, :], src).then_inc(w_in, 16)
            sp.dma_start(b_q[:, :], bq.rearrange("(d o) -> d o", o=1)).then_inc(w_in, 16)
            sp.dma_start(b_k[:, :], bk.rearrange("(d o) -> d o", o=1)).then_inc(w_in, 16)
            sp.dma_start(w_r[:, :], router_w).then_inc(w_in, 16)
            xv = x.rearrange("b (t p) d -> p (b t) d", p=P)
            for c in range(4):
                n = T // 4
                sp.dma_start(xs[:, c * n:(c + 1) * n, :], xv[:, c * n:(c + 1) * n, :]).then_inc(x_in, 16)
            sp.dma_start(b1_row[:, :], b1).then_inc(b1_in, 16)
            sp.dma_start(w_1[:, :, :], w1.rearrange("e d f -> d e f")).then_inc(w_big, 16)
            sp.dma_start(w_2[:, :, :, :], w2.rearrange("e (k p) d -> p e k d", p=P)).then_inc(w_big, 16)
            sp.wait_ge(b1_moved, 4)
            for r in range(3):
                sp.dma_start(b1_rows[r:r + 1, :, :], b1_part[:, r, :]).then_inc(w_big, 16)
            sp.wait_ge(const_pool, 2)
            for k in range(SPARE):
                r0 = E * REGION + k * P
                sp.dma_start(routed[r0:r0 + P, :], pad_rows[:, :]).then_inc(pads_in, 16)
            sp.wait_ge(pads_in, 16 * SPARE)
            sp.wait_ge(scattered, 16 * T)
            sp.wait_ge(padded, 16 * E)
            sp.wait_ge(table_ready, 2)

            def fetch(u, k):
                need(sp, stored[k], 16 * u)
                r = sp.value_load(tile_row[0:1, bass.ds(NR * u + k, 1)], min_val=0, max_val=ROWS - P)
                sp.dma_start(fr[:, k, :], routed[bass.ds(r, P), :]).then_inc(row_in[k], 16)
            for k in range(NR):
                fetch(0, k)
            with sp.Fori(1, FT // NR) as u:
                for k in range(NR):
                    fetch(u, k)
            for k in range(FT % NR):
                fetch(FT // NR, k)

        @block.gpsimd
        def _(pool):
            pool.memset(pad_rows[:, :], 0.0).then_inc(const_pool, 1)
            pool.wait_ge(const_pool, 1)
            pool.iota(pad_rows[:, 2 * D:2 * D + 1].bitcast(I32), [[0, 1]], base=NO_TOKEN,
                      channel_multiplier=1).then_inc(const_pool, 1)
            pool.memset(ident[:, :], 0.0).then_inc(const_pool, 1)
            pool.memset(before[:, :], 1.0).then_inc(const_pool, 1)
            pool.memset(ones_b[:, :], 1.0).then_inc(const_pool, 1)
            pool.memset(head_of_row[:, :], 1.0).then_inc(const_pool, 1)
            pool.memset(head_cols[:, :, :], 0.0).then_inc(const_pool, 1)
            pool.memset(km[:, :, :, :], 0.0).then_inc(const_pool, 1)
            pool.memset(v_one[:, :, :], 0.0).then_inc(const_pool, 1)
            pool.memset(v_keep[:, :, :], 0.0).then_inc(const_pool, 1)
            pool.memset(minus_half[:, :], -0.5).then_inc(const_pool, 1)
            pool.memset(zero_e[:, :], 0.0).then_inc(const_pool, 1)
            pool.wait_ge(const_pool, 12)
            pool.affine_select(out=ident[:, :], in_=ident[:, :], compare_op=ALU.not_equal, fill=1.0,
                               base=0, pattern=[[-1, P]], channel_multiplier=1).then_inc(const_pool, 1)
            pool.affine_select(out=before[:, :], in_=before[:, :], compare_op=ALU.is_gt, fill=0.0,
                               base=0, pattern=[[1, P]], channel_multiplier=-1).then_inc(const_pool, 1)
            pool.affine_select(out=head_of_row[:, :], in_=head_of_row[:, :], compare_op=ALU.is_ge, fill=0.0,
                               base=0, pattern=[[-DK, H]], channel_multiplier=1).then_inc(const_pool, 1)
            pool.wait_ge(const_pool, 15)
            pool.affine_select(out=head_of_row[:, :], in_=head_of_row[:, :], compare_op=ALU.is_ge, fill=0.0,
                               base=DK - 1, pattern=[[DK, H]], channel_multiplier=-1).then_inc(const_pool, 1)
            made = [16]

            def alone(ins):
                made[0] += 1
                ins.then_inc(const_pool, 1)
                pool.wait_ge(const_pool, made[0])

            pool.wait_ge(const_pool, made[0])
            alone(pool.affine_select(out=head_cols[0:C, :, :], in_=head_cols[0:C, :, :], compare_op=ALU.not_equal,
                                     fill=1.0, base=0, pattern=[[0, 2 * PAIRS], [-1, C]], channel_multiplier=1))
            for part in range(2):
                alone(pool.affine_select(out=head_cols[C:C + 32, :, :], in_=head_cols[C:C + 32, :, :],
                                         compare_op=ALU.not_equal, fill=1.0, base=-H * part,
                                         pattern=[[-1, H], [0, C]], channel_multiplier=1))
            for par in range(2):
                for hf in range(2):
                    r0 = C * (1 - hf)
                    v = km[r0:r0 + C, par, hf, :]
                    alone(pool.affine_select(out=v, in_=v, compare_op=ALU.not_equal, fill=1.0, base=0,
                                             pattern=[[0, H // 2], [-1, C]], channel_multiplier=1))
            for half in range(2):
                for sub in range(2):
                    hh = 2 * sub + half
                    alone(pool.memset(v_one[C * half:C * half + C, sub, DK * hh:DK * hh + DK], 1.0))
                    alone(pool.memset(v_keep[C * half:C * half + C, sub, hh:hh + 1], 1.0))
            pool.iota(rev_int[:, :], [[-1, E]], base=E, channel_multiplier=0).then_inc(const_pool, 1)
            pool.iota(region_int[:, :], [[REGION, E]], base=0, channel_multiplier=0).then_inc(const_pool, 1)
            pool.iota(token_no[:, :], [[P, T]], base=0, channel_multiplier=1).then_inc(const_pool, 1)
            pool.iota(steps_i[:, :, :], [[0, E], [P, T]], base=0, channel_multiplier=0).then_inc(const_pool, 1)
            pool.iota(tile_i[:, :, :], [[1, FT], [0, E]], base=0, channel_multiplier=0).then_inc(const_pool, 1)
            pool.iota(part_i[:, :], [[0, E]], base=0, channel_multiplier=1).then_inc(const_pool, 1)
            pool.wait_ge(tanh_done, 1)
            pool.wait_ge(w_in, W_IN)
            pool.tensor_scalar(bo_g[:, :], b_o[:, :], tanh_g[:, 0:1], None, ALU.mult).then_inc(ln1_done, 1)
            pool.wait_ge(b1_in, 16)
            pool.tensor_copy(b1_part[:, 0, :], b1_row[:, :]).then_inc(b1_moved, 1)
            pool.wait_ge(b1_moved, 1)
            pool.tensor_tensor(b1_rest[:, 0, :], b1_row[:, :], b1_part[:, 0, :], ALU.subtract).then_inc(b1_moved, 1)
            pool.wait_ge(b1_moved, 2)
            pool.tensor_copy(b1_part[:, 1, :], b1_rest[:, 0, :]).then_inc(b1_moved, 1)
            pool.wait_ge(b1_moved, 3)
            pool.tensor_tensor(b1_part[:, 2, :], b1_rest[:, 0, :], b1_part[:, 1, :], ALU.subtract).then_inc(b1_moved, 1)
            pool.wait_ge(stats_done, T + 2)
            pool.tensor_tensor(rstd1[:, 0:4], ve1[:, 0:4], minus_half[:, 0:4], ALU.pow).then_inc(rstd_done, 1)
            pool.wait_ge(setup_dve, 11)
            pool.wait_ge(const_pool, CONSTANTS)

            def front(b, par):
                need(pool, b_psum, 4 * (b - 1))
                need(pool, km_ready, 2 * (b - 1))
                pool.tensor_tensor(k_bd[:, par, :, :], kT[:, bass.ds(b, 1), :].to_broadcast([P, H, C]),
                                   head_of_row[:, :, None].to_broadcast([P, H, C]), ALU.mult).then_inc(kb_ready, 1)
                need(pool, pv_done, 4 * (b - 1))
                for s in range(2):
                    pool.tensor_tensor(
                        v_st[:, par, :, s, :].rearrange("p g (h d) -> p g h d", d=DK),
                        v_sb[:, bass.ds(b, 1), :].rearrange("p o (g h d) -> p (o g) h d", g=4, d=DK),
                        v_keep[:, s, :][:, None, :, None].to_broadcast([P, 4, 4, DK]),
                        ALU.mult).then_inc(vb_ready, 1)
                pool.wait_ge(xh_ready, 2 * b + 2)
                pool.tensor_tensor(xs[:, bass.ds(b * TB, TB), :], xs[:, bass.ds(b * TB, TB), :],
                                   bo_g[:, None, :].to_broadcast([P, TB, D]), ALU.add).then_inc(ln1_done, 1)

            def step(i, par):
                nxt = 1 - par
                if has(i + 1):
                    front(i + 1, 1 - par)
                if has(i - 1):
                    pool.wait_ge(mv2_ready, i)
                    pool.tensor_tensor(rstd2[:, :], ve2[:, :], minus_half[:, 0:TB], ALU.pow).then_inc(rstd2_ready, 1)
                    pool.tensor_copy(xr[:, nxt, :, 2 * D:2 * D + 1].bitcast(I32),
                                     token_no[:, bass.ds((i - 1) * TB, TB)][:, :, None]).then_inc(id_ready, 1)
                if has(i - 2):
                    apart(pool, const_pool)
                    pool.wait_ge(pos_ready, i - 1)
                    pool.wait_ge(xr_ready, 2 * (i - 1))
                    pool.wait_ge(id_ready, i - 1)
                    for t in range(TB):
                        pool.indirect_dma_start(
                            routed[:, :], bass.IndirectOffsetOnAxis(ap=pos[:, par, t:t + 1], axis=0),
                            xr[:, par, t, :], None, bounds_check=ROWS - 1, oob_is_err=True)\
                            .then_inc(scattered, 16)

            pool.tensor_tensor(rstd1[:, 4:T], ve1[:, 4:T], minus_half[:, 4:T], ALU.pow).then_inc(rstd_done, 1)
            steps(pool, step)
            pool.wait_ge(pad_ready, 1)
            for e in range(E):
                pool.indirect_dma_start(
                    routed[:, :], bass.IndirectOffsetOnAxis(ap=pad_i[:, e:e + 1], axis=0),
                    pad_rows[:, :], None, bounds_check=ROWS - 1, oob_is_err=True).then_inc(padded, 16)

            def store(u, k):
                apart(pool, const_pool)
                pool.wait_ge(fo_ready[k], u)
                pool.indirect_dma_start(
                    out_rows, bass.IndirectOffsetOnAxis(ap=fr[:, k, 2 * D:2 * D + 1].bitcast(I32), axis=0),
                    fo[:, k, :], None, bounds_check=N - 1, oob_is_err=False).then_inc(stored[k], 16)
            with pool.Fori(1, FT // NR + 1) as turn:
                for k in range(NR):
                    store(turn, k)
            for t in range(FT // NR * NR, FT):
                store(t // NR + 1, t % NR)
            for k in range(NR):
                pool.wait_ge(stored[k], 16 * ((FT + NR - 1 - k) // NR))

        @block.scalar
        def _(act):
            act.dma_start(gates[:, 0:1], g_xattn.rearrange("(o n) -> o n", o=1).to_broadcast([P, 1])).then_inc(w_in, 16)
            act.dma_start(gates[:, 1:2], g_ffn.rearrange("(o n) -> o n", o=1).to_broadcast([P, 1])).then_inc(w_in, 16)
            act.dma_start(b_v[:, :], bv.rearrange("(o n) -> o n", o=1).to_broadcast([P, D])).then_inc(w_in, 16)
            act.dma_start(b_o[:, :], bo.rearrange("(o n) -> o n", o=1).to_broadcast([P, D])).then_inc(w_in, 16)
            act.dma_start(b_r[:, :], router_b.rearrange("(o n) -> o n", o=1).to_broadcast([P, E])).then_inc(w_in, 16)
            act.dma_start(mask_i[:, :, :], mask.rearrange("a b (t p) c -> p (a b t) c", p=P)).then_inc(ctx_sem, 16)
            act.dma_start(b_2[:, :, :], b2.rearrange("(o e) d -> o e d", o=1).to_broadcast([P, E, D])).then_inc(w_big, 16)
            act.wait_ge(w_in, W_IN)
            act.activation(tanh_g[:, :], gates[:, :], ACT.Tanh).then_inc(tanh_done, 1)

            def keys(b, par):
                act.wait_ge(kb_ready, b + 1)
                need(act, a_psum, 2 * (b - 1))
                for hf in range(2):
                    r0 = C * hf
                    act.activation(km[r0:r0 + C, par, hf, :],
                                   k_bd[r0:r0 + C, par, hf * (H // 2):(hf + 1) * (H // 2), :]
                                   .rearrange("p h c -> p (h c)"), ACT.Copy).then_inc(km_ready, 1)

            def queries(b, par):
                act.wait_ge(q_ready, b + 1)
                need(act, a_psum, 2 * (b - 1))
                for hf in range(2):
                    act.activation(qm[C * hf:C * hf + C, par, hf, :], qT[C * hf:C * hf + C, par, :], ACT.Copy)\
                        .then_inc(qb_ready, 1)

            def shifts(b, par):
                act.wait_ge(shift_psum, b + 1)
                need(act, b_psum, 4 * (b - 1))
                act.activation(sm[C:C + 32, par, :], psR16[0:32, 512:512 + S], ACT.Copy).then_inc(sm_ready, 1)

            def exps(i, q0, q1):
                for q in range(q0, q1):
                    act.wait_ge(b_psum, 4 * i + (q + 1))
                    need(act, pv_done, 4 * (i - 1) + (q + 1))
                    act.activation(pT[:, q, :, :].rearrange("p a s -> p (a s)"),
                                   psB[:, (q % 2) * 512:(q % 2 + 1) * 512], ACT.Exp, scale=SCALE).then_inc(p_ready, 1)

            def step(i, par):
                act.wait_ge(t_psum, i + 2)
                if has(i + 1) and has(i - 2):
                    act.activation(turned[:, par, :, :].rearrange("p a s -> p (a s)"), psT[:, :], ACT.Copy)\
                        .then_inc(t_evac, 1)
                else:
                    k = 0 if has(i + 1) else 1
                    if has(i + 1) or has(i - 2):
                        act.activation(turned[:, par, k, :], psT[:, k * S:(k + 1) * S], ACT.Copy).then_inc(t_evac, 1)
                if not has(i):
                    if i == FIRST:
                        queries(0, 0)
                        keys(0, 0)
                        shifts(0, 0)
                    return
                exps(i, 0, 1)
                if has(i + 1):
                    queries(i + 1, 1 - par)
                exps(i, 1, 2)
                if has(i + 1):
                    keys(i + 1, 1 - par)
                exps(i, 2, 4)
                if has(i + 1):
                    shifts(i + 1, 1 - par)

            steps(act, step)

            def rows(t, k):
                act.wait_ge(fx_psum, t + 1)
                need(act, up_psum, t - 1)
                act.activation(fxT[:, k, :], psT[:, 0:P], ACT.Copy).then_inc(fx_ready, 1)

            def gates_of(t, k):
                act.wait_ge(up_psum, t + 1)
                need(act, hid_ready, t - 1)
                act.activation(sig[:, k, :], (psA, psB)[k][:, F:F2], ACT.Sigmoid).then_inc(sig_ready, 1)

            def hidden(t, k):
                act.wait_ge(ht_psum, t + 1)
                need(act, y_psum, t - 1)
                act.activation(hT[:, k, :], psQ[:, :], ACT.Copy).then_inc(ht_ready, 1)

            def tile(t, k):
                if not isinstance(t, int) or t + 1 < FT:
                    gates_of(t + 1, 1 - k)
                hidden(t, k)
                if not isinstance(t, int) or t + 2 < FT:
                    rows(t + 2, k)

            rows(0, 0)
            gates_of(0, 0)
            rows(1, 1)
            for t in range(4):
                tile(t, t % 2)
            with act.Fori(4, FT - 4, 2) as t:
                tile(t, 0)
                tile(t + 1, 1)
            for t in range((FT - 3) // 2 * 2, FT):
                tile(t, t % 2)

        @block.vector
        def _(dve):
            dve.wait_ge(const_pool, CONSTANTS)
            dve.tensor_copy(identb[:, :], ident[:, :]).then_inc(const_dve, 1)
            dve.tensor_copy(rev_expert[:, :], rev_int[:, :]).then_inc(const_dve, 1)
            dve.tensor_copy(region0[:, :], region_int[:, :]).then_inc(const_dve, 1)
            dve.tensor_copy(region_first[:, :], region_int[:, :]).then_inc(const_dve, 1)
            dve.tensor_copy(steps_f[:, :, :], steps_i[:, :, :]).then_inc(const_dve, 1)
            dve.tensor_copy(tile_f[:, :, :], tile_i[:, :, :]).then_inc(const_dve, 1)
            dve.tensor_copy(part_f[:, :], part_i[:, :]).then_inc(const_dve, 1)
            dve.memset(xr[:, :, :, 2 * D:], 0.0).then_inc(const_dve, 1)
            dve.wait_ge(ctx_sem, 32)
            dve.tensor_scalar(mask_b[:, :, :, :], mask_i[:, :, None, :].to_broadcast([P, TB, 2, C]), 0.0, MASKED,
                              ALU.is_equal, ALU.mult).then_inc(setup_dve, 1)
            dve.tensor_scalar(seen[:, :, :], mask_i[:, :, :], 0.0, None, ALU.not_equal).then_inc(setup_dve, 1)
            dve.wait_ge(setup_dve, 2)
            dve.tensor_reduce(some[:, :], seen[:, :, :], AX.X, ALU.max).then_inc(setup_dve, 1)
            dve.wait_ge(setup_dve, 3)
            dve.tensor_copy(some_b[:, :], some[:, :]).then_inc(setup_dve, 1)
            for c in range(2):
                dve.wait_ge(setup_pe, c + 1)
                dve.tensor_copy(ctxT[:, 8 * c:8 * c + 8, :, :],
                                (psT, psQ)[c][:, :].rearrange("p (b k) -> p b k", k=C)[:, :, None, :]
                                .to_broadcast([P, 8, 2, C])).then_inc(setup_dve, 1)
            dve.wait_ge(w_in, W_IN)
            dve.wait_ge(setup_pe, 3)
            dve.tensor_scalar(kT[:, :, :].rearrange("p b k -> p (b k)"), psA[:, :], b_k[:, 0:1], None, ALU.add)\
                .then_inc(setup_dve, 1)
            for c in range(4):
                dve.wait_ge(setup_pe, 4 + c)
                dve.tensor_tensor(v_sb[:, 4 * c:4 * c + 4, :], psB[:, (c % 2) * 512:(c % 2 + 1) * 512]
                                  .rearrange("p (b d) -> p b d", d=D), b_v[:, None, :].to_broadcast([P, 4, D]),
                                  ALU.add).then_inc(setup_dve, 1)
            dve.wait_ge(setup_pe, 8)
            for par in range(2):
                dve.tensor_copy(qm[C:P, par, 0, :], psR16[C:P, 0:S]).then_inc(setup_dve, 1)
                dve.tensor_copy(qm[0:C, par, 1, :], psR16[0:C, 0:S]).then_inc(setup_dve, 1)
                dve.tensor_copy(sm[0:C, par, :], psR16[0:C, 0:S]).then_inc(setup_dve, 1)
            dve.tensor_copy(q_keep[:, :], psO[:, 0:S]).then_inc(setup_dve, 1)
            dve.wait_ge(x_in, 64)
            with dve.Fori(0, T - 7, 8) as t:
                for k in range(8):
                    dve.bn_stats(stats[:, bass.ds(t + k, 1), :], xs[:, bass.ds(t + k, 1), :]).then_inc(stats_done, 1)
            dve.wait_ge(stats_done, T)
            for t in range(T):
                last = dve.bn_aggr(mv1[:, t, :], stats[:, t, :])
            last.then_inc(stats_done, 1)
            dve.wait_ge(stats_done, T + 1)
            dve.tensor_scalar(ve1[:, :], mv1[:, :, 1], EPS, None, ALU.add).then_inc(stats_done, 1)
            dve.wait_ge(rstd_done, 1)

            def normalize(b, par, t):
                need(dve, t_psum, b - 1)
                dve.tensor_scalar(xh[:, par, t, :], xs[:, bass.ds(b * TB + t, 1), :],
                                  mv1[:, bass.ds(b * TB + t, 1), 0:1], rstd1[:, bass.ds(b * TB + t, 1)],
                                  ALU.subtract, ALU.mult).then_inc(xh_ready, 1)

            for b in range(2):
                for t in range(TB):
                    normalize(b, b, t)
            dve.wait_ge(rstd_done, 2)

            def step(i, par):
                nxt = 1 - par
                first = isinstance(i, int) and i == FIRST
                route = []
                if has(i - 2):
                    r = 7 * (i - 2)

                    def logits():
                        dve.wait_ge(route_psum, i - 1)
                        dve.tensor_tensor(lg[:, :, :], psR[:, 0:TB * E].rearrange("p (t e) -> p t e", e=E),
                                          b_r[:, None, :].to_broadcast([P, TB, E]), ALU.add).then_inc(route_dve, 1)

                    def greatest():
                        dve.wait_ge(route_dve, r + 1)
                        dve.tensor_reduce(lmax[:, :], lg[:, :, :], AX.X, ALU.max).then_inc(route_dve, 1)

                    def equal():
                        dve.wait_ge(route_dve, r + 2)
                        dve.tensor_tensor(leq[:, :, :], lg[:, :, :], lmax[:, :, None].to_broadcast([P, TB, E]),
                                          ALU.is_equal).then_inc(route_dve, 1)

                    def reverse():
                        dve.wait_ge(route_dve, r + 3)
                        dve.tensor_tensor(lrev[:, :, :], leq[:, :, :], rev_expert[:, None, :].to_broadcast([P, TB, E]),
                                          ALU.mult).then_inc(route_dve, 1)

                    def lowest():
                        dve.wait_ge(route_dve, r + 4)
                        dve.tensor_reduce(lbest[:, :], lrev[:, :, :], AX.X, ALU.max).then_inc(route_dve, 1)

                    def hot():
                        dve.wait_ge(route_dve, r + 5)
                        dve.tensor_tensor(onehot[:, :, :], lrev[:, :, :], lbest[:, :, None].to_broadcast([P, TB, E]),
                                          ALU.is_equal).then_inc(onehot_ready, 1)
                    route = [logits, greatest, equal, reverse, lowest, hot]

                def routing():
                    if route:
                        route.pop(0)()

                if has(i + 1):
                    dve.wait_ge(q_psum, i + 2)
                    need(dve, b_psum, 4 * i)
                    need(dve, qb_ready, 2 * i)
                    dve.scalar_tensor_tensor(out=qT[:, nxt, :], in0=psQ[:, 0:S], scalar=b_q[:, 0:1],
                                             in1=q_keep[:, :], op0=ALU.add, op1=ALU.mult).then_inc(q_ready, 1)
                routing()
                if has(i + 2) and not first:
                    normalize(i + 2, par, 0)
                routing()
                if has(i + 2) and not first:
                    normalize(i + 2, par, 1)
                routing()
                if has(i - 1):
                    dve.wait_ge(wo_psum, i)
                    dve.wait_ge(ln1_done, i + 1)
                    need(dve, scattered, 32 * (i - 2))
                    dve.scalar_tensor_tensor(out=xr[:, nxt, :, 0:D], in0=psQ[:, S:2 * S].rearrange("p (t d) -> p t d", d=D),
                                             scalar=tanh_g[:, 0:1], in1=xs[:, bass.ds((i - 1) * TB, TB), :],
                                             op0=ALU.mult, op1=ALU.add).then_inc(x2_ready, 1)
                routing()
                if has(i + 1):
                    dve.wait_ge(a_psum, 2 * (i + 1) + 1)
                    dve.tensor_reduce(top[:, nxt, 0, :], psA[:, :].rearrange("p (h k) -> p h k", k=C), AX.X,
                                      ALU.max).then_inc(a_max, 1)
                routing()
                if has(i - 1):
                    dve.wait_ge(x2_ready, i)
                    for t in range(TB):
                        dve.bn_stats(st2[:, t, :], xr[:, nxt, t, 0:D]).then_inc(st2_done, 1)
                routing()
                if has(i - 1):
                    dve.wait_ge(st2_done, 4 * (i - 1) + 2)
                    need(dve, rstd2_ready, i - 1)
                    dve.memset(hold[:, :], 0.0)
                    for t in range(TB):
                        dve.bn_aggr(mv2[:, nxt, t, :], st2[:, t, :]).then_inc(st2_done, 1)
                    dve.wait_ge(st2_done, 4 * (i - 1) + 4)
                    dve.tensor_scalar(ve2[:, :], mv2[:, nxt, :, 1], EPS, None, ALU.add).then_inc(mv2_ready, 1)
                if has(i + 1):
                    dve.wait_ge(a_psum, 2 * (i + 1) + 2)
                    dve.tensor_reduce(top[:, nxt, 1, :], psA[:, :].rearrange("p (h k) -> p h k", k=C), AX.X,
                                      ALU.max).then_inc(a_max, 1)
                    dve.wait_ge(a_max, 2 * (i + 1) + 2)
                    need(dve, shift_psum, i + 1)
                    dve.tensor_scalar(shift[:, :, 0, :], top[:, nxt, :, :], -1.0, None, ALU.mult).then_inc(shift_hi, 1)
                    dve.wait_ge(shift_hi, i + 2)
                    dve.scalar_tensor_tensor(out=shift[:, :, 1, :], in0=top[:, nxt, :, :], scalar=-1.0,
                                             in1=shift[:, :, 0, :], op0=ALU.mult, op1=ALU.subtract)\
                        .then_inc(shift_ready, 1)
                if has(i - 2):
                    dve.wait_ge(rank_psum, i - 1)
                    dve.tensor_tensor(slot[:, :, :], psR[:, 32:32 + TB * E].rearrange("p (t e) -> p t e", e=E),
                                      region0[:, None, :].to_broadcast([P, TB, E]), ALU.add).then_inc(route_dve, 1)
                    dve.wait_ge(route_dve, 7 * (i - 2) + 6)
                    dve.tensor_tensor(region0[:, :], psR[:, 64:64 + E], region0[:, :], ALU.add)
                    dve.tensor_tensor(slot1[:, :, :], slot[:, :, :], onehot[:, :, :], ALU.mult).then_inc(route_dve, 1)
                if has(i - 1):
                    dve.wait_ge(rstd2_ready, i)
                    for t in range(TB):
                        dve.tensor_scalar(xr[:, nxt, t, D:2 * D], xr[:, nxt, t, 0:D], mv2[:, nxt, t, 0:1],
                                          rstd2[:, t:t + 1], ALU.subtract, ALU.mult).then_inc(xr_ready, 1)
                if has(i - 2):
                    dve.wait_ge(route_dve, 7 * (i - 2) + 7)
                    need(dve, scattered, 32 * (i - 3))
                    with nc.allow_low_precision(reason="row numbers: integers below 2**24"):
                        dve.tensor_reduce(pos[:, par, :], slot1[:, :, :], AX.X, ALU.add).then_inc(pos_ready, 1)
                if has(i):
                    dve.wait_ge(pv_done, 4 * i + 4)
                    need(dve, o_ready, i)
                    dve.reciprocal(inv[:, :], psO[:, S:2 * S]).then_inc(inv_ready, 1)
                    dve.wait_ge(inv_ready, i + 1)
                    need(dve, wo_psum, i)
                    dve.tensor_tensor(oT[:, :], psO[:, 0:S], inv[:, :], ALU.mult).then_inc(o_ready, 1)

            steps(dve, step)

            dve.wait_ge(pos_ready, B)
            chain = [0]

            def link(ins):
                chain[0] += 1
                ins.then_inc(table_dve, 1)
                dve.wait_ge(table_dve, chain[0])
            dve.tensor_tensor(pad_i[:, :], part_f[:, :], region0[:, :], ALU.add).then_inc(pad_ready, 1)
            link(dve.tensor_tensor(count[:, :], region0[0:1, :], region_first[0:1, :], ALU.subtract))
            link(dve.tensor_tensor(over[:, :, :], count[:, :, None].to_broadcast([1, E, T]), steps_f[:, :, :], ALU.is_gt))
            link(dve.tensor_reduce(ntile[:, :], over[:, :, :], AX.X, ALU.add))
            link(dve.tensor_tensor_scan(cum[:, :], ntile[:, :], zero_e[:, :], 0.0, ALU.add, ALU.add))
            link(dve.tensor_scalar(jump[:, :], ntile[:, :], -float(P), float(REGION), ALU.mult, ALU.add))
            link(dve.tensor_tensor(past[:, :, :], tile_f[:, :, :], cum[:, None, :].to_broadcast([1, FT, E]), ALU.is_ge))
            link(dve.tensor_tensor(jumps[:, :, :], past[:, :, :], jump[:, None, :].to_broadcast([1, FT, E]), ALU.mult))
            link(dve.tensor_reduce(e_sum[:, :], past[:, :, :], AX.X, ALU.add))
            link(dve.tensor_reduce(r_sum[:, :], jumps[:, :, :], AX.X, ALU.add))
            dve.tensor_scalar(tile_expert[:, :], e_sum[:, :], float(E - 1), None, ALU.min).then_inc(table_ready, 1)
            dve.scalar_tensor_tensor(out=tile_row[:, :], in0=tile_f[:, :, 0], scalar=float(P), in1=r_sum[:, :],
                                     op0=ALU.mult, op1=ALU.add).then_inc(table_ready, 1)

            dve.wait_ge(table_ready, 2)

            def gate(t, k):
                dve.wait_ge(sig_ready, t + 1)
                need(dve, ht_psum, t - 1)
                dve.tensor_tensor(hid[:, k, :], (psA, psB)[k][:, 0:F], sig[:, k, :], ALU.mult).then_inc(hid_ready, 1)

            def finish(u, k):
                t = NR * u + k
                e = dve.value_load(tile_expert[0:1, bass.ds(t, 1)], min_val=0, max_val=E - 1)
                dve.wait_ge(y_psum, t + 1)
                dve.tensor_tensor(yb[:, k % 2, :], psO[:, 0:D], b_2[:, bass.ds(e, 1), :].rearrange("p o d -> p (o d)"),
                                  ALU.add).then_inc(yb_ready, 1)
                dve.wait_ge(yb_ready, t + 1)
                need(dve, stored[k], 16 * u)
                dve.scalar_tensor_tensor(out=fo[:, k, :], in0=yb[:, k % 2, :], scalar=tanh_g[:, 1:2],
                                         in1=fr[:, k, 0:D], op0=ALU.mult, op1=ALU.add).then_inc(fo_ready[k], 1)

            gate(0, 0)
            dve.wait_ge(w_big, 96)
            for t in range(NR + 1):
                gate(t + 1, (t + 1) % 2)
                if t > 0:
                    finish((t - 1) // NR, (t - 1) % NR)
            with dve.Fori(1, FT // NR) as u:
                for k in range(NR):
                    gate(NR * u + (k + 2), k % 2)
                    finish(u, k)
            for t in range(FT // NR * NR + 1, FT + 1):
                if t + 1 < FT:
                    gate(t + 1, (t + 1) % 2)
                finish((t - 1) // NR, (t - 1) % NR)

        @block.tensor
        def _(pe):
            pe.wait_ge(const_pool, CONSTANTS)
            pe.wait_ge(ctx_sem, 32)
            for c in range(2):
                for k in range(4):
                    last = pe.transpose((psT, psQ)[c][:, k * P:(k + 1) * P], ctx_sb[:, 4 * c + k, :], ident[:, :])
                last.then_inc(setup_pe, 1)
            pe.wait_ge(w_in, W_IN)
            for c in range(2):
                pe.wait_ge(setup_dve, 5 + c)
                last = pe.matmul(psA[:, c * 512:(c + 1) * 512], w_k[:, :], ctxT[:, 8 * c:8 * c + 8, 0, :],
                                 start=True, stop=True)
            last.then_inc(setup_pe, 1)
            for c in range(4):
                if c >= 2:
                    pe.wait_ge(setup_dve, 8 + c - 2)
                for k in range(4):
                    b = 4 * c + k
                    col = (c % 2) * 512 + k * D
                    last = pe.matmul(psB[:, col:col + D], ctxT[:, b, :, :].rearrange("p a k -> p (a k)"), w_v[:, :],
                                     start=True, stop=True)
                last.then_inc(setup_pe, 1)
            pe.wait_ge(setup_dve, 4)
            pe.wait_ge(const_dve, 1)
            for t in range(TB):
                pe.transpose(psR16[:, t * P:(t + 1) * P], mask_b[:, t, :, :].rearrange("p a k -> p (a k)"), identb[:, :])
            for t in range(TB):
                last = pe.matmul(psO[:, t * P:(t + 1) * P], some_b[:, t:t + 1].to_broadcast([P, P]), identb[:, :],
                                 start=True, stop=True)
            last.then_inc(setup_pe, 1)

            def step(i, par):
                nxt = 1 - par

                def scores(q):
                    need(pe, p_ready, 4 * i + (q + 1) - 2)
                    for k in range(2):
                        p = 2 * q + k
                        o = psB[:, (q % 2) * 512 + k * S:(q % 2) * 512 + (k + 1) * S]
                        pe.matmul(o, k_bd[:, par, 2 * p:2 * p + 2, :].rearrange("p h k -> p (h k)"), qT[:, par, :],
                                  start=True, stop=False)
                        last = pe.matmul(o, head_cols[0:C + 32, p, :], sm[:, par, :], start=False, stop=True)
                    last.then_inc(b_psum, 1)

                def values(q):
                    pe.wait_ge(p_ready, 4 * i + (q + 1))
                    if q == 0:
                        need(pe, o_ready, i)
                        pe.wait_ge(vb_ready, 2 * i + 2)
                    rows = slice(32 * q, 32 * q + 32)
                    for k in range(2):
                        pe.matmul(psO[rows, 0:S], v_st[:, par, q, k, :], pT[:, q, k, :], start=(k == 0), stop=(k == 1),
                                  tile_position=(0, 32 * q))
                    for k in range(2):
                        last = pe.matmul(psO[rows, S:2 * S], v_one[:, k, :], pT[:, q, k, :], start=(k == 0),
                                         stop=(k == 1), tile_position=(0, 32 * q))
                    last.then_inc(pv_done, 1)

                def maxima(t):
                    need(pe, a_max, 2 * (i + 1) + t)
                    for hf in range(2):
                        last = pe.matmul(psA[:, hf * HALF:(hf + 1) * HALF], qm[:, nxt, hf, t * P:(t + 1) * P],
                                         km[:, nxt, hf, :], start=True, stop=True)
                    last.then_inc(a_psum, 1)

                need(pe, t_evac, i + 1)
                last = None
                if has(i + 1):
                    pe.wait_ge(xh_ready, 2 * (i + 2))
                    for t in range(TB):
                        last = pe.transpose(psT[:, t * P:(t + 1) * P], xh[:, nxt, t, :], ident[:, :])
                if has(i - 2):
                    pe.wait_ge(xr_ready, 2 * (i - 1))
                    for t in range(TB):
                        last = pe.transpose(psT[:, S + t * P:S + (t + 1) * P], xr[:, par, t, D:2 * D], ident[:, :])
                last.then_inc(t_psum, 1)
                if has(i):
                    pe.wait_ge(sm_ready, i + 1)
                    pe.wait_ge(kb_ready, i + 1)
                    scores(0)
                if has(i + 1):
                    pe.wait_ge(t_evac, i + 2)
                    need(pe, x2_ready, i - 1)
                    pe.matmul(psQ[:, 0:S], w_q[:, :], turned[:, par, 0, :], start=True, stop=True).then_inc(q_psum, 1)
                if has(i):
                    scores(1)
                if has(i - 2):
                    pe.wait_ge(t_evac, i + 2)
                    need(pe, sm_ready, min(i + 1, B) if isinstance(i, int) else i + 1)
                    need(pe, pos_ready, i - 2)
                    for t in range(TB):
                        last = pe.matmul(psR[:, t * E:(t + 1) * E], turned[:, par, 1, t * P:(t + 1) * P], w_r[:, :],
                                         start=True, stop=True)
                    last.then_inc(route_psum, 1)
                if has(i):
                    values(0)
                if has(i - 1):
                    pe.wait_ge(o_ready, i)
                    need(pe, q_ready, min(i + 2, B) if isinstance(i, int) else i + 2)
                    for t in range(TB):
                        last = pe.matmul(psQ[:, S + t * D:S + (t + 1) * D], oT[:, t * P:(t + 1) * P], w_o[:, :],
                                         start=True, stop=True)
                    last.then_inc(wo_psum, 1)
                if has(i + 1):
                    pe.wait_ge(qb_ready, 2 * (i + 2))
                    pe.wait_ge(km_ready, 2 * (i + 2))
                    maxima(0)
                if has(i):
                    scores(2)
                    values(1)
                if has(i + 1):
                    maxima(1)
                if has(i - 2):
                    pe.wait_ge(onehot_ready, i - 1)
                    for t in range(TB):
                        pe.matmul(psR[:, 32 + t * E:32 + (t + 1) * E], before[:, :], onehot[:, t, :], start=(t == 0),
                                  stop=False, skip_group_check=True)
                    pe.matmul(psR[:, 32 + E:32 + 2 * E], ones_b[:, :], onehot[:, 0, :], start=False, stop=True,
                              skip_group_check=True)
                    for t in range(TB):
                        last = pe.matmul(psR[:, 64:64 + E], ones_b[:, :], onehot[:, t, :], start=False,
                                         stop=(t == TB - 1), skip_group_check=True)
                    last.then_inc(rank_psum, 1)
                if has(i):
                    scores(3)
                    values(2)
                    values(3)
                if has(i + 1):
                    pe.wait_ge(shift_ready, i + 2)
                    need(pe, pos_ready, i - 1)
                    for t in range(TB):
                        last = pe.transpose(psR16[0:32, 512 + t * P:512 + (t + 1) * P],
                                            shift[:, t, :, :].rearrange("p a h -> p (a h)"), identb[:, :])
                    last.then_inc(shift_psum, 1)

            pe.wait_ge(setup_dve, 18)
            steps(pe, step)

            pe.wait_ge(table_ready, 2)
            pe.wait_ge(w_big, 96)

            def turn(u, j):
                u, j = u + j // NR, j % NR
                pe.wait_ge(row_in[j], 16 * u + 16)
                need(pe, fx_ready, NR * u + j)
                pe.transpose(psT[:, 0:P], fr[:, j, D:2 * D], ident[:, :]).then_inc(fx_psum, 1)

            def up(t, k):
                ps = (psA, psB)[k]
                e = pe.value_load(tile_expert[0:1, bass.ds(t, 1)], min_val=0, max_val=E - 1)
                pe.wait_ge(fx_ready, t + 1)
                need(pe, hid_ready, t - 1)
                for c in (1, 0):
                    o = ps[:, c * F:(c + 1) * F]
                    pe.matmul(o, ones_b[0:3, :], b1_rows[:, bass.ds(e, 1), c * F:(c + 1) * F], start=True, stop=False)
                    last = pe.matmul(o, fxT[:, k, :], w_1[:, bass.ds(e, 1), c * F:(c + 1) * F], start=False, stop=True)
                last.then_inc(up_psum, 1)

            def flip(t, k):
                pe.wait_ge(hid_ready, t + 1)
                need(pe, ht_ready, t)
                for f in range(FB):
                    last = pe.transpose(psQ[:, f * P:(f + 1) * P], hid[:, k, f * P:(f + 1) * P], ident[:, :])
                last.then_inc(ht_psum, 1)

            def down(t, k):
                e = pe.value_load(tile_expert[0:1, bass.ds(t, 1)], min_val=0, max_val=E - 1)
                pe.wait_ge(ht_ready, t + 1)
                need(pe, yb_ready, t)
                for f in range(FB):
                    last = pe.matmul(psO[:, 0:D], hT[:, k, f * P:(f + 1) * P],
                                     w_2[:, bass.ds(e, 1), f:f + 1, :], start=(f == 0), stop=(f == FB - 1))
                last.then_inc(y_psum, 1)

            turn(0, 0)
            up(0, 0)
            turn(0, 1)

            def tile(u, j):
                t, k = NR * u + j, j % 2
                inside = not isinstance(t, int)
                if inside or t + 1 < FT:
                    up(t + 1, 1 - k)
                flip(t, k)
                if inside or t + 2 < FT:
                    turn(u, j + 2)
                if inside or t > 0:
                    down(t - 1, 1 - k)

            for j in range(NR):
                tile(0, j)
            with pe.Fori(1, FT // NR) as u:
                for j in range(NR):
                    tile(u, j)
            for j in range(FT % NR):
                tile(FT // NR, j)
            down(FT - 1, (FT - 1) % 2)


_INS = ['x', 'ctx_1024', 'mask_1x1xSxS2_ik0', 'g_xattn', 'g_ffn', 'L0_xattn_wq', 'L0_xattn_bq', 'L0_xattn_wk',
        'L0_xattn_bk', 'L0_xattn_wv', 'L0_xattn_bv', 'L0_xattn_wo', 'L0_xattn_bo', 'L0_ffn_router_w',
        'L0_ffn_router_b', 'L0_ffn_w1', 'L0_ffn_b1', 'L0_ffn_w2', 'L0_ffn_b2']


def kernel(**inputs):
    import numpy as _np
    import concourse.bacc as _bacc
    from concourse import mybir as _mybir
    from concourse.bass_utils import run_bass_kernel_spmd as _run

    nc = _bacc.Bacc("TRN2", target_bir_lowering=False, num_devices=1)
    arrays, args = {}, []
    for name in _INS:
        a = _np.ascontiguousarray(inputs[name])
        arrays[f"in_{name}_dram"] = a
        args.append(nc.dram_tensor(f"in_{name}_dram", a.shape, _mybir.dt.from_np(a.dtype), kind="ExternalInput").ap())
    shape = inputs['x'].shape
    out = nc.dram_tensor("out_0_dram", shape, _mybir.dt.float32, kind="ExternalOutput").ap()
    gated_xattn_moe(nc, *args, out)
    r = _run(nc, [arrays], core_ids=[0])
    return r.results[0]["out_0_dram"]
```

```python
from contextlib import ExitStack

import concourse.bass as bass
from concourse import mybir

ALU = mybir.AluOpType
ACT = mybir.ActivationFunctionType
AX = mybir.AxisListType
F32 = mybir.dt.float32
F32R = mybir.dt.float32r
BF16 = mybir.dt.bfloat16
I32 = mybir.dt.int32

P = 128
MASKED = -(2.0 ** 100)


def need(eng, sem, value):
    if isinstance(value, int) and value <= 0:
        return
    eng.wait_ge(sem, value)


def apart(eng, reached):
    eng.wait_ge(reached, 1)


def gated_xattn_moe(nc, x, ctx_in, mask, g_xattn, g_ffn, wq, bq, wk, bk, wv, bv, wo, bo,
                    router_w, router_b, w1, b1, w2, b2, out):
    B, S, D = x.shape
    C = ctx_in.shape[1]
    H = 16
    DK = D // H
    E = router_w.shape[1]
    F2 = w1.shape[2]
    F = F2 // 2
    FB = F // P
    TB = S // P
    T = B * TB
    N = B * S
    G = 4
    HG = H // G
    SLOT = P // 4
    PAIRS = H // 2
    HC = H * C
    HALF = HC // 2
    SCALE = float(DK) ** -0.5
    EPS = 1e-5

    ROW = 2 * D + 8
    REGION = N + P
    FT = T + E - 1
    SPARE = FT - T
    ROWS = E * REGION + SPARE * P
    NO_TOKEN = 2 * N

    routed = nc.dram_tensor("routed_rows", (ROWS, ROW), F32, kind="Internal").ap()
    k_dram = nc.dram_tensor("k_parts", (2, D, B * C), F32, kind="Internal").ap()
    q_dram = nc.dram_tensor("q_parts", (2, 2, D // G, G, S), F32, kind="Internal").ap()
    out_rows = out.rearrange("b s d -> (b s) d")

    with ExitStack() as stack:
        def sb(name, shape, dt=F32):
            return stack.enter_context(nc.sbuf_tensor("sb_" + name, shape, dt))

        def sem(name):
            return stack.enter_context(nc.semaphore(name))

        ident = sb("ident", [P, P])
        identb = sb("identb", [P, P], BF16)
        before = sb("before", [P, P], BF16)
        ones_b = sb("ones_b", [P, P], BF16)
        head_of_row = sb("head_of_row", [P, H])
        head_of_slot = sb("head_of_slot", [P, HG])
        v_keep = sb("v_keep", [P, 2, 4])
        head_cols = sb("head_cols", [P, PAIRS, P], BF16)
        rev_expert = sb("rev_expert", [P, E])
        rev_int = sb("rev_int", [P, E], I32)
        region0 = sb("region0", [P, E])
        region_int = sb("region_int", [P, E], I32)
        region_first = sb("region_first", [P, E])
        token_no = sb("token_no", [P, T], I32)
        pad_rows = sb("pad_rows", [P, ROW])
        minus_half = sb("minus_half", [P, T])
        w_q = sb("w_q", [P, D])
        w_k = sb("w_k", [P, D])
        w_v = sb("w_v", [P, D])
        w_o = sb("w_o", [P, D])
        w_r = sb("w_r", [P, E])
        b_q = sb("b_q", [P, 1])
        b_k = sb("b_k", [P, 1])
        b_v = sb("b_v", [P, D])
        b_o = sb("b_o", [P, D])
        b_r = sb("b_r", [P, E])
        gates = sb("gates", [P, 2])
        tanh_g = sb("tanh_g", [P, 2])
        bo_g = sb("bo_g", [P, D])
        w_1 = sb("w_1", [P, E, F2])
        w_2 = sb("w_2", [P, E, FB, D])
        b_2 = sb("b_2", [P, E, D])
        b1_rows = sb("b1_rows", [3, E, F2], BF16)
        xs = sb("xs", [P, T, D])
        ctx_sb = sb("ctx_sb", [P, B // 2, D])
        ctxT = sb("ctxT", [P, B, 2, C])
        b1_row = ctxT[0:E, 0:B // 2, :, :].rearrange("p b a c -> p (b a c)")
        b1_rest = ctxT[0:E, B // 2:B, :, :].rearrange("p b a c -> p (b a c)")
        kT = sb("kT", [P, B, C])
        k_slots = sb("k_slots", [P, G, B, C], F32R)
        v_sb = sb("v_sb", [P, B, D])
        mask_i = sb("mask_i", [P, TB, C], I32)
        mask_b = sb("mask_b", [P, TB, 2, C], BF16)
        seen = sb("seen", [P, TB, C])
        some = sb("some", [P, TB])
        some_b = sb("some_b", [P, TB], BF16)
        q_keep = sb("q_keep", [P, S])
        stats = sb("stats", [P, T, 6])
        mv1 = sb("mv1", [P, T, 2])
        ve1 = sb("ve1", [P, T])
        rstd1 = sb("rstd1", [P, T])
        xh = sb("xh", [P, 2, TB, D])
        turned = sb("turned", [P, 2, 2, S])
        qT = sb("qT", [P, 2, S])
        q_parts = sb("q_parts", [P, 2, 2, S], F32R)
        q_slots = sb("q_slots", [P, 2, G, S], F32R)
        qm = sb("qm", [P, 2, 2, S], BF16)
        k_bd = sb("k_bd", [P, 2, H, C], F32R)
        km = sb("km", [P, 2, 2, HALF], BF16)
        v_st = sb("v_st", [P, 2, 4, 2, 32])
        v_one = sb("v_one", [P, 2, 32])
        top = sb("top", [P, 2, TB, H])
        shift = sb("shift", [P, TB, 2, H], BF16)
        sm = sb("sm", [96, 2, S], BF16)
        pT = sb("pT", [P, 4, 2, S])
        inv = sb("inv", [P, S])
        oT = sb("oT", [P, S])
        xr = sb("xr", [P, 2, TB, ROW])
        st2 = sb("st2", [P, TB, 6])
        mv2 = sb("mv2", [P, 2, TB, 2])
        ve2 = sb("ve2", [P, TB])
        rstd2 = sb("rstd2", [P, TB])
        hold = sb("hold", [1, 1])
        lg = sb("lg", [P, TB, E])
        lmax = sb("lmax", [P, TB])
        leq = sb("leq", [P, TB, E])
        lrev = sb("lrev", [P, TB, E])
        lbest = sb("lbest", [P, TB])
        onehot = sb("onehot", [P, TB, E], BF16)
        slot = sb("slot", [P, TB, E])
        slot1 = sb("slot1", [P, TB, E])
        pos = sb("pos", [P, 2, TB], I32)
        count = sb("count", [1, E])
        steps_i = sb("steps_i", [1, E, T], I32)
        steps_f = sb("steps_f", [1, E, T])
        over = sb("over", [1, E, T])
        ntile = sb("ntile", [1, E])
        cum = sb("cum", [1, E])
        zero_e = sb("zero_e", [1, E])
        jump = sb("jump", [1, E])
        tile_i = sb("tile_i", [1, FT, E], I32)
        tile_f = sb("tile_f", [1, FT, E])
        past = sb("past", [1, FT, E])
        jumps = sb("jumps", [1, FT, E])
        e_sum = sb("e_sum", [1, FT])
        r_sum = sb("r_sum", [1, FT])
        tile_expert = sb("tile_expert", [1, FT], I32)
        tile_row = sb("tile_row", [1, FT], I32)
        pad_i = sb("pad_i", [P, E], I32)
        part_i = sb("part_i", [P, E], I32)
        part_f = sb("part_f", [P, E])
        NR = 6
        fr = sb("fr", [P, NR, ROW])
        b1_part = fr[:, :, :].rearrange("p n r -> p (n r)")[0:E, :].bitcast(BF16)[:, 0:3 * F2]\
            .rearrange("p (r f) -> p r f", r=3)
        fxT = sb("fxT", [P, 2, P])
        pT_flat = pT[:, :, :, :].rearrange("p q a s -> p q (a s)")
        sig, hid = pT_flat[:, 0:2, :], pT_flat[:, 2:4, :]
        hT = kT[:, :, :].rearrange("p b c -> p (b c)").rearrange("p (a f) -> p a f", a=2)
        k_parts = pT_flat.rearrange("p (r a) f -> p r (a f)", r=2).bitcast(F32R)
        yb = sb("yb", [P, 2, D])
        fo = ctx_sb[:, 0:NR, :]

        def bank(name, n=1):
            return stack.enter_context(nc.psum_tensor("ps_" + name, [P, n * 512], F32))

        psA = bank("A", 2)
        psB = bank("B", 2)
        psO = bank("O")
        psT = bank("T")
        psQ = bank("Q")
        psR = bank("R")
        psR16 = psR[:, :].bitcast(BF16)
        psT16 = psT[:, :].bitcast(BF16)

        w_in, w_big, ctx_sem, b1_in, b1_moved = (sem(n) for n in (
            "w_in", "w_big", "ctx_in_sem", "b1_in", "b1_moved"))
        x_in = [sem(f"x_in{c}") for c in range(4)]
        const_pool, const_dve = sem("const_pool"), sem("const_dve")
        pads_in = sem("pads_in")
        setup_pe, setup_dve, setup_act = sem("setup_pe"), sem("setup_dve"), sem("setup_act")
        stats_done, rstd_done, ln1_done = sem("stats_done"), sem("rstd_done"), sem("ln1_done")
        tanh_done = sem("tanh_done")
        rstd2_ready, id_ready = sem("rstd2_ready"), sem("id_ready")
        k_high, k_low, k_out_first, k_out, k_in_first, k_in, q_out, qh_ready, ql_ready = (
            sem(n) for n in ("k_high", "k_low", "k_out_first", "k_out", "k_in_first", "k_in", "q_out", "qh_ready", "ql_ready"))
        q_in = [sem(f"q_in{par}") for par in range(2)]
        kb_ready, km_ready, vb_ready, qb_ready = sem("kb_ready"), sem("km_ready"), sem("vb_ready"), sem("qb_ready")
        xh_ready, t_psum, t_evac = sem("xh_ready"), sem("t_psum"), sem("t_evac")
        q_psum, q_ready = sem("q_psum"), sem("q_ready")
        a_psum, a_max = sem("a_psum"), sem("a_max")
        shift_hi, shift_ready, shift_psum, sm_ready = (sem(n) for n in (
            "shift_hi", "shift_ready", "shift_psum", "sm_ready"))
        b_psum, p_ready, pv_done = sem("b_psum"), sem("p_ready"), sem("pv_done")
        inv_ready, o_ready = sem("inv_ready"), sem("o_ready")
        wo_psum, x2_ready = sem("wo_psum"), sem("x2_ready")
        st2_done, mv2_ready, xr_ready = sem("st2_done"), sem("mv2_ready"), sem("xr_ready")
        route_psum, route_dve, onehot_ready, rank_psum, pos_ready = (sem(n) for n in (
            "route_psum", "route_dve", "onehot_ready", "rank_psum", "pos_ready"))
        scattered = sem("scattered")
        table_dve, table_pool, table_ready, pad_ready = (sem(n) for n in (
            "table_dve", "table_pool", "table_ready", "pad_ready"))
        padded = sem("padded")
        row_in = [sem(f"row_in{k}") for k in range(NR)]
        stored = [sem(f"stored{k}") for k in range(NR)]
        fo_ready = [sem(f"fo_ready{k}") for k in range(NR)]
        fx_psum, fx_ready, up_psum, sig_ready, hid_ready, ht_psum, ht_ready, y_psum, yb_ready = (
            sem(n) for n in ("fx_psum", "fx_ready", "up_psum", "sig_ready", "hid_ready", "ht_psum",
                             "ht_ready", "y_psum", "yb_ready"))

        W_IN = 12 * 16
        EARLY = 3 * TB
        W_PARTS = 4
        W_BIG = (2 * W_PARTS + 4) * 16
        IDENT, HEAD_OF_ROW = 2, 7
        CONSTANTS = 35
        block = stack.enter_context(nc.Block())

        FIRST, LAST = -2, B + 1
        LOOP0, LOOP1 = 4, B - 4

        def steps(eng, step):
            for i in range(FIRST, LOOP0):
                step(i, i % 2)
            with eng.Fori(LOOP0, LOOP1 - 1, 2) as i:
                step(i, 0)
                step(i + 1, 1)
            for i in range(LOOP1, LAST + 1):
                step(i, i % 2)

        def has(b):
            return not isinstance(b, int) or 0 <= b < B

        @block.sync
        def _(sp):
            sp.dma_start(ctx_sb[:, :, :], ctx_in.rearrange("(a b) k d -> (b k) a d", b=2)).then_inc(ctx_sem, 16)
            for dst, src in ((w_k, wk), (w_v, wv), (w_q, wq), (w_o, wo)):
                sp.dma_start(dst[:, :], src).then_inc(w_in, 16)
            sp.dma_start(b_q[:, :], bq.rearrange("(d o) -> d o", o=1)).then_inc(w_in, 16)
            sp.dma_start(b_k[:, :], bk.rearrange("(d o) -> d o", o=1)).then_inc(w_in, 16)
            sp.dma_start(w_r[:, :], router_w).then_inc(w_in, 16)
            xv = x.rearrange("b (t p) d -> p (b t) d", p=P)
            for c in range(4):
                n = T // 4
                sp.dma_start(xs[:, c * n:(c + 1) * n, :], xv[:, c * n:(c + 1) * n, :]).then_inc(x_in[c], 16)
            sp.wait_ge(k_high, 1)
            sp.wait_ge(k_low, 1)
            for b0, b_end, away in ((0, 2, k_out_first), (2, B, k_out)):
                sp.dma_start(k_dram[:, :, b0 * C:b_end * C].rearrange("r p c -> p r c"),
                             k_parts[:, :, b0 * C:b_end * C].bitcast(F32)).then_inc(away, 16)
            for b0, b_end, away, done in ((0, 2, k_out_first, k_in_first), (2, B, k_out, k_in)):
                sp.wait_ge(away, 16)
                for r in range(2):
                    for s in range(2):
                        row = (2 * r + s) * SLOT
                        sp.dma_start(k_slots[row:row + SLOT, :, b0:b_end, :].bitcast(F32),
                                     k_dram[r, :, b0 * C:b_end * C].rearrange("(g r) c -> r g c", g=G))\
                            .then_inc(done, 16)
            sp.wait_ge(setup_pe, 8)
            sp.dma_start(b1_row[:, :], b1).then_inc(b1_in, 16)
            sp.wait_ge(const_pool, CONSTANTS)
            for k in range(SPARE):
                r0 = E * REGION + k * P
                sp.dma_start(routed[r0:r0 + P, :], pad_rows[:, :]).then_inc(pads_in, 16)

            def step(i, par):
                if has(i + 2):
                    for r, ready in enumerate((qh_ready, ql_ready)):
                        sp.wait_ge(ready, i + 3)
                        sp.dma_start(q_dram[par, r].rearrange("r g s -> g r s"),
                                     q_parts[:, par, r, :].bitcast(F32)).then_inc(q_out, 16)
                    sp.wait_ge(q_out, 32 * (i + 3))
                    sp.dma_start(q_slots[:, par, :, :].bitcast(F32),
                                 q_dram[par:par + 1].rearrange("o t r g s -> o (t r) (g s)")
                                 .to_broadcast([2, 2 * SLOT, G * S])).then_inc(q_in[par], 16)
                if isinstance(i, int) and 0 <= i < W_PARTS:
                    n = E // W_PARTS
                    sp.dma_start(w_1[:, i * n:(i + 1) * n, :],
                                 w1.rearrange("e d f -> d e f")[:, i * n:(i + 1) * n, :]).then_inc(w_big, 16)
                    sp.dma_start(w_2[:, i * n:(i + 1) * n, :, :],
                                 w2.rearrange("e (k p) d -> p e k d", p=P)[:, i * n:(i + 1) * n, :, :])\
                        .then_inc(w_big, 16)

            steps(sp, step)
            sp.wait_ge(b1_moved, 4)
            for r in range(3):
                sp.dma_start(b1_rows[r:r + 1, :, :], b1_part[:, r, :]).then_inc(w_big, 16)
            sp.wait_ge(pads_in, 16 * SPARE)
            sp.wait_ge(scattered, 16 * T)
            sp.wait_ge(padded, 16 * E)
            sp.wait_ge(table_ready, 2)
            sp.wait_ge(w_big, W_BIG)

            def fetch(u, k):
                need(sp, stored[k], 16 * u)
                r = sp.value_load(tile_row[0:1, bass.ds(NR * u + k, 1)], min_val=0, max_val=ROWS - P)
                sp.dma_start(fr[:, k, :], routed[bass.ds(r, P), :]).then_inc(row_in[k], 16)
            for k in range(NR):
                fetch(0, k)
            with sp.Fori(1, FT // NR) as u:
                for k in range(NR):
                    fetch(u, k)
            for k in range(FT % NR):
                fetch(FT // NR, k)

        @block.gpsimd
        def _(pool):
            pool.memset(ident[:, :], 0.0).then_inc(const_pool, 1)
            pool.wait_ge(const_pool, 1)
            pool.affine_select(out=ident[:, :], in_=ident[:, :], compare_op=ALU.not_equal, fill=1.0,
                               base=0, pattern=[[-1, P]], channel_multiplier=1).then_inc(const_pool, 1)
            pool.memset(head_of_row[:, :], 1.0).then_inc(const_pool, 1)
            pool.memset(before[:, :], 1.0).then_inc(const_pool, 1)
            pool.memset(pad_rows[:, :], 0.0).then_inc(const_pool, 1)
            pool.wait_ge(const_pool, 5)
            pool.affine_select(out=head_of_row[:, :], in_=head_of_row[:, :], compare_op=ALU.is_ge, fill=0.0,
                               base=0, pattern=[[-DK, H]], channel_multiplier=1).then_inc(const_pool, 1)
            pool.wait_ge(const_pool, 6)
            pool.affine_select(out=head_of_row[:, :], in_=head_of_row[:, :], compare_op=ALU.is_ge, fill=0.0,
                               base=DK - 1, pattern=[[DK, H]], channel_multiplier=-1).then_inc(const_pool, 1)
            pool.affine_select(out=before[:, :], in_=before[:, :], compare_op=ALU.is_gt, fill=0.0,
                               base=0, pattern=[[1, P]], channel_multiplier=-1).then_inc(const_pool, 1)
            pool.iota(pad_rows[:, 2 * D:2 * D + 1].bitcast(I32), [[0, 1]], base=NO_TOKEN,
                      channel_multiplier=1).then_inc(const_pool, 1)
            pool.memset(ones_b[:, :], 1.0).then_inc(const_pool, 1)
            pool.memset(v_one[:, :, :], 0.0).then_inc(const_pool, 1)
            pool.memset(v_keep[:, :, :], 0.0).then_inc(const_pool, 1)
            pool.memset(minus_half[:, :], -0.5).then_inc(const_pool, 1)
            pool.memset(zero_e[:, :], 0.0).then_inc(const_pool, 1)
            made = [14]

            def alone(ins):
                made[0] += 1
                ins.then_inc(const_pool, 1)
                pool.wait_ge(const_pool, made[0])

            pool.wait_ge(const_pool, made[0])
            pool.wait_ge(const_dve, 2)
            alone(pool.affine_select(out=head_cols[0:C, :, :], in_=head_cols[0:C, :, :], compare_op=ALU.not_equal,
                                     fill=1.0, base=0, pattern=[[0, 2 * PAIRS], [-1, C]], channel_multiplier=1))
            for part in range(2):
                alone(pool.affine_select(out=head_cols[C:C + 32, :, :], in_=head_cols[C:C + 32, :, :],
                                         compare_op=ALU.not_equal, fill=1.0, base=-H * part,
                                         pattern=[[-1, H], [0, C]], channel_multiplier=1))
            for par in range(2):
                for hf in range(2):
                    r0 = C * (1 - hf)
                    v = km[r0:r0 + C, par, hf, :]
                    alone(pool.affine_select(out=v, in_=v, compare_op=ALU.not_equal, fill=1.0, base=0,
                                             pattern=[[0, H // 2], [-1, C]], channel_multiplier=1))
            for half in range(2):
                for sub in range(2):
                    hh = 2 * sub + half
                    alone(pool.memset(v_one[C * half:C * half + C, sub, DK * hh:DK * hh + DK], 1.0))
                    alone(pool.memset(v_keep[C * half:C * half + C, sub, hh:hh + 1], 1.0))
            pool.iota(rev_int[:, :], [[-1, E]], base=E, channel_multiplier=0).then_inc(const_pool, 1)
            pool.iota(region_int[:, :], [[REGION, E]], base=0, channel_multiplier=0).then_inc(const_pool, 1)
            pool.iota(token_no[:, :], [[P, T]], base=0, channel_multiplier=1).then_inc(const_pool, 1)
            pool.iota(steps_i[:, :, :], [[0, E], [P, T]], base=0, channel_multiplier=0).then_inc(const_pool, 1)
            pool.iota(tile_i[:, :, :], [[1, FT], [0, E]], base=0, channel_multiplier=0).then_inc(const_pool, 1)
            pool.iota(part_i[:, :], [[0, E]], base=0, channel_multiplier=1).then_inc(const_pool, 1)
            pool.wait_ge(tanh_done, 1)
            pool.wait_ge(w_in, W_IN)
            pool.tensor_scalar(bo_g[:, :], b_o[:, :], tanh_g[:, 0:1], None, ALU.mult).then_inc(ln1_done, 1)
            pool.wait_ge(stats_done, 2 * EARLY + 1)
            pool.tensor_tensor(rstd1[:, 0:EARLY], ve1[:, 0:EARLY], minus_half[:, 0:EARLY], ALU.pow).then_inc(rstd_done, 1)
            pool.wait_ge(const_pool, CONSTANTS)

            def spread_k(b, par):
                need(pool, b_psum, 4 * (b - 1))
                need(pool, km_ready, 4 * (b - 1))
                if isinstance(b, int) and b == 0:
                    pool.wait_ge(k_in_first, 64)
                    pool.wait_ge(const_dve, 4)
                if isinstance(b, int) and b == 2:
                    pool.wait_ge(k_in, 64)
                pool.tensor_tensor(k_bd[:, par, :, :].rearrange("p (g h) c -> p g h c", g=G),
                                   k_slots[:, :, bass.ds(b, 1), :].bitcast(F32).to_broadcast([P, G, HG, C]),
                                   head_of_slot[:, None, :, None].to_broadcast([P, G, HG, C]), ALU.mult)\
                    .then_inc(kb_ready, 1)

            def front(b, par):
                need(pool, pv_done, b - 1)
                if isinstance(b, int) and b == 0:
                    pool.wait_ge(setup_dve, 11)
                for s in range(2):
                    pool.tensor_tensor(
                        v_st[:, par, :, s, :].rearrange("p g (h d) -> p g h d", d=DK),
                        v_sb[:, bass.ds(b, 1), :].rearrange("p o (g h d) -> p (o g) h d", g=4, d=DK),
                        v_keep[:, s, :][:, None, :, None].to_broadcast([P, 4, 4, DK]),
                        ALU.mult).then_inc(vb_ready, 1)
                pool.wait_ge(xh_ready, 2 * b + 2)
                pool.tensor_tensor(xs[:, bass.ds(b * TB, TB), :], xs[:, bass.ds(b * TB, TB), :],
                                   bo_g[:, None, :].to_broadcast([P, TB, D]), ALU.add).then_inc(ln1_done, 1)

            def low(b, par):
                pool.wait_ge(qh_ready, b + 1)
                pool.tensor_tensor(q_parts[:, par, 1, :], qT[:, par, :], q_parts[:, par, 0, :].bitcast(F32),
                                   ALU.subtract).then_inc(ql_ready, 1)

            def step(i, par):
                nxt = 1 - par
                if has(i + 1):
                    front(i + 1, 1 - par)
                if has(i + 2):
                    spread_k(i + 2, par)
                    low(i + 2, par)
                if has(i - 1):
                    pool.wait_ge(mv2_ready, i)
                    pool.tensor_tensor(rstd2[:, :], ve2[:, :], minus_half[:, 0:TB], ALU.pow).then_inc(rstd2_ready, 1)
                    pool.tensor_copy(xr[:, nxt, :, 2 * D:2 * D + 1].bitcast(I32),
                                     token_no[:, bass.ds((i - 1) * TB, TB)][:, :, None]).then_inc(id_ready, 1)
                if has(i - 2):
                    apart(pool, const_pool)
                    pool.wait_ge(pos_ready, i - 1)
                    pool.wait_ge(xr_ready, 2 * (i - 1))
                    pool.wait_ge(id_ready, i - 1)
                    for t in range(TB):
                        pool.indirect_dma_start(
                            routed[:, :], bass.IndirectOffsetOnAxis(ap=pos[:, par, t:t + 1], axis=0),
                            xr[:, par, t, :], None, bounds_check=ROWS - 1, oob_is_err=True)\
                            .then_inc(scattered, 16)
                if isinstance(i, int) and i == -1:
                    pool.wait_ge(stats_done, 2 * T + 2)
                    pool.tensor_tensor(rstd1[:, EARLY:T], ve1[:, EARLY:T], minus_half[:, EARLY:T], ALU.pow)\
                        .then_inc(rstd_done, 1)
                if isinstance(i, int) and i == 1:
                    pool.wait_ge(b1_moved, 1)
                    pool.tensor_tensor(b1_rest[:, :], b1_row[:, :], b1_part[:, 0, :], ALU.subtract).then_inc(b1_moved, 1)
                if isinstance(i, int) and i == 3:
                    pool.wait_ge(b1_moved, 3)
                    pool.tensor_tensor(b1_part[:, 2, :], b1_rest[:, :], b1_part[:, 1, :], ALU.subtract)\
                        .then_inc(b1_moved, 1)

            steps(pool, step)
            pool.wait_ge(pad_ready, 1)
            for e in range(E):
                pool.indirect_dma_start(
                    routed[:, :], bass.IndirectOffsetOnAxis(ap=pad_i[:, e:e + 1], axis=0),
                    pad_rows[:, :], None, bounds_check=ROWS - 1, oob_is_err=True).then_inc(padded, 16)

            def store(u, k):
                apart(pool, const_pool)
                pool.wait_ge(fo_ready[k], u)
                pool.indirect_dma_start(
                    out_rows, bass.IndirectOffsetOnAxis(ap=fr[:, k, 2 * D:2 * D + 1].bitcast(I32), axis=0),
                    fo[:, k, :], None, bounds_check=N - 1, oob_is_err=False).then_inc(stored[k], 16)
            with pool.Fori(1, FT // NR + 1) as turn:
                for k in range(NR):
                    store(turn, k)
            for t in range(FT // NR * NR, FT):
                store(t // NR + 1, t % NR)
            for k in range(NR):
                pool.wait_ge(stored[k], 16 * ((FT + NR - 1 - k) // NR))

        @block.scalar
        def _(act):
            act.dma_start(gates[:, 0:1], g_xattn.rearrange("(o n) -> o n", o=1).to_broadcast([P, 1])).then_inc(w_in, 16)
            act.dma_start(gates[:, 1:2], g_ffn.rearrange("(o n) -> o n", o=1).to_broadcast([P, 1])).then_inc(w_in, 16)
            act.dma_start(b_v[:, :], bv.rearrange("(o n) -> o n", o=1).to_broadcast([P, D])).then_inc(w_in, 16)
            act.dma_start(b_o[:, :], bo.rearrange("(o n) -> o n", o=1).to_broadcast([P, D])).then_inc(w_in, 16)
            act.dma_start(b_r[:, :], router_b.rearrange("(o n) -> o n", o=1).to_broadcast([P, E])).then_inc(w_in, 16)
            act.dma_start(mask_i[:, :, :], mask.rearrange("a b (t p) c -> p (a b t) c", p=P)).then_inc(ctx_sem, 16)
            act.dma_start(b_2[:, :, :], b2.rearrange("(o e) d -> o e d", o=1).to_broadcast([P, E, D])).then_inc(w_big, 16)
            act.wait_ge(w_in, W_IN)
            act.activation(tanh_g[:, :], gates[:, :], ACT.Tanh).then_inc(tanh_done, 1)

            act.wait_ge(setup_dve, 7)
            act.activation(k_parts[:, 0, :], kT[:, :, :].rearrange("p b c -> p (b c)"), ACT.Copy).then_inc(k_high, 1)

            def high(b, par):
                act.wait_ge(q_ready, b + 1)
                need(act, q_out, 32 * (b - 1))
                act.activation(q_parts[:, par, 0, :], qT[:, par, :], ACT.Copy).then_inc(qh_ready, 1)

            def keys(b, par):
                act.wait_ge(kb_ready, b + 1)
                need(act, a_psum, 2 * (b - 1))
                for g in range(G):
                    act.activation(km[g * SLOT:(g + 1) * SLOT, par, g // 2, (g % 2) * HG * C:(g % 2 + 1) * HG * C],
                                   k_bd[0:SLOT, par, g * HG:(g + 1) * HG, :].bitcast(F32)
                                   .rearrange("p h c -> p (h c)"), ACT.Copy).then_inc(km_ready, 1)

            def queries(b, par):
                act.wait_ge(q_ready, b + 1)
                need(act, a_psum, 2 * (b - 1))
                for hf in range(2):
                    act.activation(qm[C * hf:C * hf + C, par, hf, :], qT[C * hf:C * hf + C, par, :], ACT.Copy)\
                        .then_inc(qb_ready, 1)

            def shifts(b, par):
                act.wait_ge(shift_psum, b + 1)
                need(act, b_psum, 4 * (b - 1))
                act.activation(sm[C:C + 32, par, :], psT16[0:32, 0:S], ACT.Copy).then_inc(sm_ready, 1)

            def exps(i, q0, q1):
                for q in range(q0, q1):
                    act.wait_ge(b_psum, 4 * i + (q + 1))
                    need(act, pv_done, i)
                    act.activation(pT[:, q, :, :].rearrange("p a s -> p (a s)"),
                                   psB[:, (q % 2) * 512:(q % 2 + 1) * 512], ACT.Exp, scale=SCALE).then_inc(p_ready, 1)

            def step(i, par):
                if has(i):
                    exps(i, 0, 1)
                act.wait_ge(t_psum, i + 3)
                if has(i + 2) and has(i - 2):
                    act.activation(turned[:, par, :, :].rearrange("p a s -> p (a s)"), psT[:, :], ACT.Copy)\
                        .then_inc(t_evac, 1)
                else:
                    k = 0 if has(i + 2) else 1
                    act.activation(turned[:, par, k, :], psT[:, k * S:(k + 1) * S], ACT.Copy).then_inc(t_evac, 1)
                if has(i):
                    exps(i, 1, 3)
                if has(i + 2):
                    high(i + 2, par)
                if has(i):
                    exps(i, 3, 4)
                if has(i + 2):
                    queries(i + 2, par)
                if has(i + 1):
                    shifts(i + 1, 1 - par)
                if has(i + 2):
                    keys(i + 2, par)
                if isinstance(i, int) and i == 0:
                    act.wait_ge(b1_in, 16)
                    act.activation(b1_part[:, 0, :], b1_row[:, :], ACT.Copy).then_inc(b1_moved, 1)
                if isinstance(i, int) and i == 2:
                    act.wait_ge(b1_moved, 2)
                    act.activation(b1_part[:, 1, :], b1_rest[:, :], ACT.Copy).then_inc(b1_moved, 1)

            steps(act, step)

            def rows(t, k):
                act.wait_ge(fx_psum, t + 1)
                need(act, up_psum, t - 1)
                act.activation(fxT[:, k, :], psT[:, 0:P], ACT.Copy).then_inc(fx_ready, 1)

            def gates_of(t, k):
                act.wait_ge(up_psum, t + 1)
                need(act, hid_ready, t - 1)
                act.activation(sig[:, k, :], (psA, psB)[k][:, F:F2], ACT.Sigmoid).then_inc(sig_ready, 1)

            def hidden(t, k):
                act.wait_ge(ht_psum, t + 1)
                need(act, y_psum, t - 1)
                act.activation(hT[:, k, :], psQ[:, :], ACT.Copy).then_inc(ht_ready, 1)

            def tile(t, k):
                if not isinstance(t, int) or t + 1 < FT:
                    gates_of(t + 1, 1 - k)
                hidden(t, k)
                if not isinstance(t, int) or t + 2 < FT:
                    rows(t + 2, k)

            rows(0, 0)
            gates_of(0, 0)
            rows(1, 1)
            for t in range(4):
                tile(t, t % 2)
            with act.Fori(4, FT - 4, 2) as t:
                tile(t, 0)
                tile(t + 1, 1)
            for t in range((FT - 3) // 2 * 2, FT):
                tile(t, t % 2)

        @block.vector
        def _(dve):
            dve.memset(head_cols[:, :, :], 0.0).then_inc(const_dve, 1)
            dve.memset(km[:, :, :, :], 0.0).then_inc(const_dve, 1)
            dve.wait_ge(const_pool, IDENT)
            dve.tensor_copy(identb[:, :], ident[:, :]).then_inc(const_dve, 1)
            dve.wait_ge(const_pool, HEAD_OF_ROW)
            dve.tensor_reduce(head_of_slot[:, :], head_of_row[:, :].rearrange("p (s h) -> p h s", h=HG), AX.X, ALU.add)\
                .then_inc(const_dve, 1)
            dve.memset(xr[:, :, :, 2 * D:], 0.0).then_inc(const_dve, 1)
            dve.wait_ge(ctx_sem, 32)
            dve.tensor_scalar(mask_b[:, :, :, :], mask_i[:, :, None, :].to_broadcast([P, TB, 2, C]), 0.0, MASKED,
                              ALU.is_equal, ALU.mult).then_inc(setup_dve, 1)
            dve.tensor_scalar(seen[:, :, :], mask_i[:, :, :], 0.0, None, ALU.not_equal).then_inc(setup_dve, 1)
            dve.wait_ge(setup_dve, 2)
            dve.tensor_reduce(some[:, :], seen[:, :, :], AX.X, ALU.max).then_inc(setup_dve, 1)
            dve.wait_ge(setup_dve, 3)
            dve.tensor_copy(some_b[:, :], some[:, :]).then_inc(setup_dve, 1)
            for c in range(2):
                dve.wait_ge(setup_pe, c + 1)
                dve.tensor_copy(ctxT[:, 8 * c:8 * c + 8, :, :],
                                (psT, psQ)[c][:, :].rearrange("p (b k) -> p b k", k=C)[:, :, None, :]
                                .to_broadcast([P, 8, 2, C])).then_inc(setup_dve, 1)
            for c in range((EARLY + T // 4 - 1) // (T // 4)):
                dve.wait_ge(x_in[c], 16)
            for t in range(EARLY):
                dve.bn_stats(stats[:, t, :], xs[:, t, :]).then_inc(stats_done, 1)
            dve.wait_ge(stats_done, EARLY)
            for t in range(EARLY):
                dve.bn_aggr(mv1[:, t, :], stats[:, t, :]).then_inc(stats_done, 1)
            dve.wait_ge(stats_done, 2 * EARLY)
            dve.tensor_scalar(ve1[:, 0:EARLY], mv1[:, 0:EARLY, 1], EPS, None, ALU.add).then_inc(stats_done, 1)
            dve.wait_ge(w_in, W_IN)
            dve.wait_ge(setup_pe, 3)
            dve.tensor_scalar(kT[:, :, :].rearrange("p b k -> p (b k)"), psA[:, :], b_k[:, 0:1], None, ALU.add)\
                .then_inc(setup_dve, 1)
            dve.wait_ge(k_high, 1)
            dve.wait_ge(setup_dve, 7)
            dve.tensor_tensor(k_parts[:, 1, :], kT[:, :, :].rearrange("p b c -> p (b c)"), k_parts[:, 0, :].bitcast(F32),
                              ALU.subtract).then_inc(k_low, 1)
            for c in range(4):
                dve.wait_ge(setup_pe, 4 + c)
                dve.tensor_tensor(v_sb[:, 4 * c:4 * c + 4, :], psB[:, (c % 2) * 512:(c % 2 + 1) * 512]
                                  .rearrange("p (b d) -> p b d", d=D), b_v[:, None, :].to_broadcast([P, 4, D]),
                                  ALU.add).then_inc(setup_dve, 1)
            dve.wait_ge(setup_pe, 8)
            for par in range(2):
                dve.tensor_copy(qm[C:P, par, 0, :], psR16[C:P, 0:S]).then_inc(setup_dve, 1)
                dve.tensor_copy(qm[0:C, par, 1, :], psR16[0:C, 0:S]).then_inc(setup_dve, 1)
                dve.tensor_copy(sm[0:C, par, :], psR16[0:C, 0:S]).then_inc(setup_dve, 1)
            dve.tensor_copy(q_keep[:, :], psO[:, 0:S]).then_inc(setup_dve, 1)
            dve.wait_ge(rstd_done, 1)

            def normalize(b, par, t):
                need(dve, t_psum, b - 1)
                dve.tensor_scalar(xh[:, par, t, :], xs[:, bass.ds(b * TB + t, 1), :],
                                  mv1[:, bass.ds(b * TB + t, 1), 0:1], rstd1[:, bass.ds(b * TB + t, 1)],
                                  ALU.subtract, ALU.mult).then_inc(xh_ready, 1)

            for t in range(TB):
                normalize(0, 0, t)

            def late_stats():
                for c in range(4):
                    dve.wait_ge(x_in[c], 16)
                n = (T - EARLY) // 2
                with dve.Fori(EARLY, T - n + 1, n) as t:
                    for k in range(n):
                        dve.bn_stats(stats[:, bass.ds(t + k, 1), :], xs[:, bass.ds(t + k, 1), :]).then_inc(stats_done, 1)
                dve.wait_ge(stats_done, EARLY + T + 1)
                for t in range(EARLY, T):
                    dve.bn_aggr(mv1[:, t, :], stats[:, t, :]).then_inc(stats_done, 1)
                dve.wait_ge(stats_done, 2 * T + 1)
                dve.tensor_scalar(ve1[:, EARLY:T], mv1[:, EARLY:T, 1], EPS, None, ALU.add).then_inc(stats_done, 1)
                dve.wait_ge(const_pool, CONSTANTS)
                dve.tensor_copy(rev_expert[:, :], rev_int[:, :]).then_inc(const_dve, 1)
                dve.tensor_copy(region0[:, :], region_int[:, :]).then_inc(const_dve, 1)
                dve.tensor_copy(region_first[:, :], region_int[:, :]).then_inc(const_dve, 1)
                dve.tensor_copy(steps_f[:, :, :], steps_i[:, :, :]).then_inc(const_dve, 1)
                dve.tensor_copy(tile_f[:, :, :], tile_i[:, :, :]).then_inc(const_dve, 1)
                dve.tensor_copy(part_f[:, :], part_i[:, :]).then_inc(const_dve, 1)

            def step(i, par):
                nxt = 1 - par
                route = []
                if has(i - 2):
                    r = 7 * (i - 2)

                    def logits():
                        dve.wait_ge(route_psum, i - 1)
                        dve.tensor_tensor(lg[:, :, :], psR[:, 0:TB * E].rearrange("p (t e) -> p t e", e=E),
                                          b_r[:, None, :].to_broadcast([P, TB, E]), ALU.add).then_inc(route_dve, 1)

                    def greatest():
                        dve.wait_ge(route_dve, r + 1)
                        dve.tensor_reduce(lmax[:, :], lg[:, :, :], AX.X, ALU.max).then_inc(route_dve, 1)

                    def equal():
                        dve.wait_ge(route_dve, r + 2)
                        dve.tensor_tensor(leq[:, :, :], lg[:, :, :], lmax[:, :, None].to_broadcast([P, TB, E]),
                                          ALU.is_equal).then_inc(route_dve, 1)

                    def reverse():
                        dve.wait_ge(route_dve, r + 3)
                        dve.tensor_tensor(lrev[:, :, :], leq[:, :, :], rev_expert[:, None, :].to_broadcast([P, TB, E]),
                                          ALU.mult).then_inc(route_dve, 1)

                    def lowest():
                        dve.wait_ge(route_dve, r + 4)
                        dve.tensor_reduce(lbest[:, :], lrev[:, :, :], AX.X, ALU.max).then_inc(route_dve, 1)

                    def hot():
                        dve.wait_ge(route_dve, r + 5)
                        dve.tensor_tensor(onehot[:, :, :], lrev[:, :, :], lbest[:, :, None].to_broadcast([P, TB, E]),
                                          ALU.is_equal).then_inc(onehot_ready, 1)
                    route = [logits, greatest, equal, reverse, lowest, hot]

                def routing():
                    if route:
                        route.pop(0)()

                def maximum(t):
                    dve.wait_ge(a_psum, 2 * (i + 1) + (t + 1))
                    dve.tensor_reduce(top[:, nxt, t, :], psA[:, :].rearrange("p (h k) -> p h k", k=C), AX.X,
                                      ALU.max).then_inc(a_max, 1)

                if has(i + 1):
                    maximum(0)
                if has(i + 2):
                    dve.wait_ge(q_psum, i + 3)
                    need(dve, ql_ready, i + 1)
                    need(dve, qb_ready, 2 * (i + 1))
                    dve.scalar_tensor_tensor(out=qT[:, par, :], in0=psR[:, S:2 * S], scalar=b_q[:, 0:1],
                                             in1=q_keep[:, :], op0=ALU.add, op1=ALU.mult).then_inc(q_ready, 1)
                routing()
                if has(i + 1):
                    maximum(1)
                routing()
                if has(i + 1):
                    dve.wait_ge(a_max, 2 * (i + 1) + 2)
                    need(dve, shift_psum, i + 1)
                    dve.tensor_scalar(shift[:, :, 0, :], top[:, nxt, :, :], -1.0, None, ALU.mult).then_inc(shift_hi, 1)
                routing()
                if has(i + 1):
                    dve.wait_ge(shift_hi, i + 2)
                    dve.scalar_tensor_tensor(out=shift[:, :, 1, :], in0=top[:, nxt, :, :], scalar=-1.0,
                                             in1=shift[:, :, 0, :], op0=ALU.mult, op1=ALU.subtract)\
                        .then_inc(shift_ready, 1)
                routing()
                if has(i - 1):
                    dve.wait_ge(wo_psum, i)
                    dve.wait_ge(ln1_done, i + 1)
                    need(dve, scattered, 32 * (i - 2))
                    dve.scalar_tensor_tensor(out=xr[:, nxt, :, 0:D], in0=psQ[:, 0:S].rearrange("p (t d) -> p t d", d=D),
                                             scalar=tanh_g[:, 0:1], in1=xs[:, bass.ds((i - 1) * TB, TB), :],
                                             op0=ALU.mult, op1=ALU.add).then_inc(x2_ready, 1)
                routing()
                if isinstance(i, int) and i == 0:
                    dve.wait_ge(rstd_done, 2)
                if has(i + 3):
                    normalize(i + 3, nxt, 0)
                routing()
                if has(i - 1):
                    dve.wait_ge(x2_ready, i)
                    for t in range(TB):
                        dve.bn_stats(st2[:, t, :], xr[:, nxt, t, 0:D]).then_inc(st2_done, 1)
                if has(i + 3):
                    normalize(i + 3, nxt, 1)
                if has(i - 1):
                    dve.wait_ge(st2_done, 4 * (i - 1) + 2)
                    need(dve, rstd2_ready, i - 1)
                    dve.memset(hold[:, :], 0.0)
                    for t in range(TB):
                        dve.bn_aggr(mv2[:, nxt, t, :], st2[:, t, :]).then_inc(st2_done, 1)
                    dve.wait_ge(st2_done, 4 * (i - 1) + 4)
                    dve.tensor_scalar(ve2[:, :], mv2[:, nxt, :, 1], EPS, None, ALU.add).then_inc(mv2_ready, 1)
                if has(i - 2):
                    dve.wait_ge(rank_psum, i - 1)
                    dve.tensor_tensor(slot[:, :, :], psR[:, 32:32 + TB * E].rearrange("p (t e) -> p t e", e=E),
                                      region0[:, None, :].to_broadcast([P, TB, E]), ALU.add).then_inc(route_dve, 1)
                    dve.wait_ge(route_dve, 7 * (i - 2) + 6)
                    dve.tensor_tensor(region0[:, :], psR[:, 64:64 + E], region0[:, :], ALU.add)
                    dve.tensor_tensor(slot1[:, :, :], slot[:, :, :], onehot[:, :, :], ALU.mult).then_inc(route_dve, 1)
                    dve.wait_ge(route_dve, 7 * (i - 2) + 7)
                    need(dve, scattered, 32 * (i - 3))
                    with nc.allow_low_precision(reason="row numbers: integers below 2**24"):
                        dve.tensor_reduce(pos[:, par, :], slot1[:, :, :], AX.X, ALU.add).then_inc(pos_ready, 1)
                if has(i - 1):
                    dve.wait_ge(rstd2_ready, i)
                    for t in range(TB):
                        dve.tensor_scalar(xr[:, nxt, t, D:2 * D], xr[:, nxt, t, 0:D], mv2[:, nxt, t, 0:1],
                                          rstd2[:, t:t + 1], ALU.subtract, ALU.mult).then_inc(xr_ready, 1)
                if has(i):
                    dve.wait_ge(pv_done, i + 1)
                    need(dve, o_ready, i)
                    dve.reciprocal(inv[:, :], psO[:, S:2 * S]).then_inc(inv_ready, 1)
                if has(i):
                    dve.wait_ge(inv_ready, i + 1)
                    need(dve, wo_psum, i)
                    dve.tensor_tensor(oT[:, :], psO[:, 0:S], inv[:, :], ALU.mult).then_inc(o_ready, 1)

                if isinstance(i, int) and i == FIRST:
                    late_stats()

            steps(dve, step)

            dve.wait_ge(pos_ready, B)
            chain = [0]

            def link(ins):
                chain[0] += 1
                ins.then_inc(table_dve, 1)
                dve.wait_ge(table_dve, chain[0])
            dve.tensor_tensor(pad_i[:, :], part_f[:, :], region0[:, :], ALU.add).then_inc(pad_ready, 1)
            link(dve.tensor_tensor(count[:, :], region0[0:1, :], region_first[0:1, :], ALU.subtract))
            link(dve.tensor_tensor(over[:, :, :], count[:, :, None].to_broadcast([1, E, T]), steps_f[:, :, :], ALU.is_gt))
            link(dve.tensor_reduce(ntile[:, :], over[:, :, :], AX.X, ALU.add))
            link(dve.tensor_tensor_scan(cum[:, :], ntile[:, :], zero_e[:, :], 0.0, ALU.add, ALU.add))
            link(dve.tensor_scalar(jump[:, :], ntile[:, :], -float(P), float(REGION), ALU.mult, ALU.add))
            link(dve.tensor_tensor(past[:, :, :], tile_f[:, :, :], cum[:, None, :].to_broadcast([1, FT, E]), ALU.is_ge))
            link(dve.tensor_tensor(jumps[:, :, :], past[:, :, :], jump[:, None, :].to_broadcast([1, FT, E]), ALU.mult))
            link(dve.tensor_reduce(e_sum[:, :], past[:, :, :], AX.X, ALU.add))
            link(dve.tensor_reduce(r_sum[:, :], jumps[:, :, :], AX.X, ALU.add))
            dve.tensor_scalar(tile_expert[:, :], e_sum[:, :], float(E - 1), None, ALU.min).then_inc(table_ready, 1)
            dve.scalar_tensor_tensor(out=tile_row[:, :], in0=tile_f[:, :, 0], scalar=float(P), in1=r_sum[:, :],
                                     op0=ALU.mult, op1=ALU.add).then_inc(table_ready, 1)

            dve.wait_ge(table_ready, 2)

            def gate(t, k):
                dve.wait_ge(sig_ready, t + 1)
                need(dve, ht_psum, t - 1)
                dve.tensor_tensor(hid[:, k, :], (psA, psB)[k][:, 0:F], sig[:, k, :], ALU.mult).then_inc(hid_ready, 1)

            def finish(u, k):
                t = NR * u + k
                e = dve.value_load(tile_expert[0:1, bass.ds(t, 1)], min_val=0, max_val=E - 1)
                dve.wait_ge(y_psum, t + 1)
                dve.tensor_tensor(yb[:, k % 2, :], psO[:, 0:D], b_2[:, bass.ds(e, 1), :].rearrange("p o d -> p (o d)"),
                                  ALU.add).then_inc(yb_ready, 1)
                dve.wait_ge(yb_ready, t + 1)
                need(dve, stored[k], 16 * u)
                dve.scalar_tensor_tensor(out=fo[:, k, :], in0=yb[:, k % 2, :], scalar=tanh_g[:, 1:2],
                                         in1=fr[:, k, 0:D], op0=ALU.mult, op1=ALU.add).then_inc(fo_ready[k], 1)

            gate(0, 0)
            dve.wait_ge(w_big, W_BIG)
            for t in range(NR + 1):
                gate(t + 1, (t + 1) % 2)
                if t > 0:
                    finish((t - 1) // NR, (t - 1) % NR)
            with dve.Fori(1, FT // NR) as u:
                for k in range(NR):
                    gate(NR * u + (k + 2), k % 2)
                    finish(u, k)
            for t in range(FT // NR * NR + 1, FT + 1):
                if t + 1 < FT:
                    gate(t + 1, (t + 1) % 2)
                finish((t - 1) // NR, (t - 1) % NR)

        @block.tensor
        def _(pe):
            pe.wait_ge(const_pool, IDENT)
            pe.wait_ge(ctx_sem, 32)
            for c in range(2):
                for k in range(4):
                    last = pe.transpose((psT, psQ)[c][:, k * P:(k + 1) * P], ctx_sb[:, 4 * c + k, :], ident[:, :])
                last.then_inc(setup_pe, 1)
            pe.wait_ge(w_in, W_IN)
            for c in range(2):
                pe.wait_ge(setup_dve, 5 + c)
                last = pe.matmul(psA[:, c * 512:(c + 1) * 512], w_k[:, :], ctxT[:, 8 * c:8 * c + 8, 0, :],
                                 start=True, stop=True)
            last.then_inc(setup_pe, 1)
            for c in range(4):
                if c >= 2:
                    pe.wait_ge(setup_dve, 8 + c - 2)
                for k in range(4):
                    b = 4 * c + k
                    col = (c % 2) * 512 + k * D
                    last = pe.matmul(psB[:, col:col + D], ctxT[:, b, :, :].rearrange("p a k -> p (a k)"), w_v[:, :],
                                     start=True, stop=True)
                last.then_inc(setup_pe, 1)
            pe.wait_ge(setup_dve, 4)
            pe.wait_ge(const_dve, 3)
            for t in range(TB):
                pe.transpose(psR16[:, t * P:(t + 1) * P], mask_b[:, t, :, :].rearrange("p a k -> p (a k)"), identb[:, :])
            for t in range(TB):
                last = pe.matmul(psO[:, t * P:(t + 1) * P], some_b[:, t:t + 1].to_broadcast([P, P]), identb[:, :],
                                 start=True, stop=True)
            last.then_inc(setup_pe, 1)

            def step(i, par):
                nxt = 1 - par

                def scores(q):
                    need(pe, p_ready, 4 * i + (q + 1) - 2)
                    for k in range(2):
                        p = 2 * q + k
                        o = psB[:, (q % 2) * 512 + k * S:(q % 2) * 512 + (k + 1) * S]
                        pe.matmul(o, k_bd[:, par, 2 * p:2 * p + 2, :].rearrange("p h k -> p (h k)"),
                                  q_slots[:, par, q, :],
                                  start=True, stop=False)
                        last = pe.matmul(o, head_cols[0:C + 32, p, :], sm[:, par, :], start=False, stop=True)
                    last.then_inc(b_psum, 1)

                def values():
                    pe.wait_ge(p_ready, 4 * i + 4)
                    need(pe, o_ready, i)
                    pe.wait_ge(vb_ready, 2 * i + 2)
                    for c in range(2):
                        for k in range(2):
                            for g in range(G):
                                rows = slice(SLOT * g, SLOT * g + SLOT)
                                kept = (v_st[:, par, g, k, :], v_one[:, k, :])[c]
                                last = pe.matmul(psO[rows, c * S:(c + 1) * S], kept, pT[:, g, k, :], start=(k == 0),
                                                 stop=(k == 1), tile_position=(0, SLOT * g))
                    last.then_inc(pv_done, 1)

                def maxima(t):
                    need(pe, a_max, 2 * (i + 1) + t)
                    for hf in range(2):
                        last = pe.matmul(psA[:, hf * HALF:(hf + 1) * HALF], qm[:, nxt, hf, t * P:(t + 1) * P],
                                         km[:, nxt, hf, :], start=True, stop=True)
                    last.then_inc(a_psum, 1)

                if has(i):
                    pe.wait_ge(sm_ready, i + 1)
                    pe.wait_ge(kb_ready, i + 1)
                    pe.wait_ge(q_in[par], 8 * (i + (2 - par)))
                    scores(0)
                need(pe, t_evac, i + 2)
                need(pe, sm_ready, min(i + 1, B) if isinstance(i, int) else i + 1)
                last = None
                if has(i + 2):
                    pe.wait_ge(xh_ready, 2 * (i + 3))
                    for t in range(TB):
                        last = pe.transpose(psT[:, t * P:(t + 1) * P], xh[:, par, t, :], ident[:, :])
                if has(i - 2):
                    pe.wait_ge(xr_ready, 2 * (i - 1))
                    for t in range(TB):
                        last = pe.transpose(psT[:, S + t * P:S + (t + 1) * P], xr[:, par, t, D:2 * D], ident[:, :])
                last.then_inc(t_psum, 1)
                if has(i + 1):
                    pe.wait_ge(qb_ready, 2 * (i + 2))
                    pe.wait_ge(km_ready, 4 * (i + 2))
                    maxima(0)
                if has(i):
                    scores(1)
                pe.wait_ge(t_evac, i + 3)
                need(pe, pos_ready, i - 2)
                if has(i - 2):
                    for t in range(TB):
                        last = pe.matmul(psR[:, t * E:(t + 1) * E], turned[:, par, 1, t * P:(t + 1) * P], w_r[:, :],
                                         start=True, stop=True)
                    last.then_inc(route_psum, 1)
                if has(i + 2):
                    pe.matmul(psR[:, S:2 * S], w_q[:, :], turned[:, par, 0, :], start=True, stop=True).then_inc(q_psum, 1)
                if has(i + 1):
                    maxima(1)
                if has(i):
                    scores(2)
                    scores(3)
                if has(i - 1):
                    pe.wait_ge(o_ready, i)
                    need(pe, x2_ready, i - 1)
                    for t in range(TB):
                        last = pe.matmul(psQ[:, t * D:(t + 1) * D], oT[:, t * P:(t + 1) * P], w_o[:, :],
                                         start=True, stop=True)
                    last.then_inc(wo_psum, 1)
                if has(i + 1):
                    pe.wait_ge(shift_ready, i + 2)
                    for t in range(TB):
                        last = pe.transpose(psT16[0:32, t * P:(t + 1) * P],
                                            shift[:, t, :, :].rearrange("p a h -> p (a h)"), identb[:, :])
                    last.then_inc(shift_psum, 1)
                if has(i - 2):
                    pe.wait_ge(onehot_ready, i - 1)
                    if has(i + 2):
                        pe.wait_ge(q_ready, i + 3)
                    for t in range(TB):
                        pe.matmul(psR[:, 32 + t * E:32 + (t + 1) * E], before[:, :], onehot[:, t, :], start=(t == 0),
                                  stop=False, skip_group_check=True)
                    pe.matmul(psR[:, 32 + E:32 + 2 * E], ones_b[:, :], onehot[:, 0, :], start=False, stop=True,
                              skip_group_check=True)
                    for t in range(TB):
                        last = pe.matmul(psR[:, 64:64 + E], ones_b[:, :], onehot[:, t, :], start=False,
                                         stop=(t == TB - 1), skip_group_check=True)
                    last.then_inc(rank_psum, 1)
                if has(i):
                    values()

            pe.wait_ge(setup_dve, 18)
            pe.wait_ge(const_pool, CONSTANTS)
            steps(pe, step)

            pe.wait_ge(table_ready, 2)
            pe.wait_ge(w_big, W_BIG)

            def turn(u, j):
                u, j = u + j // NR, j % NR
                pe.wait_ge(row_in[j], 16 * u + 16)
                need(pe, fx_ready, NR * u + j)
                pe.transpose(psT[:, 0:P], fr[:, j, D:2 * D], ident[:, :]).then_inc(fx_psum, 1)

            def up(t, k):
                ps = (psA, psB)[k]
                e = pe.value_load(tile_expert[0:1, bass.ds(t, 1)], min_val=0, max_val=E - 1)
                pe.wait_ge(fx_ready, t + 1)
                need(pe, hid_ready, t - 1)
                for c in (1, 0):
                    o = ps[:, c * F:(c + 1) * F]
                    pe.matmul(o, ones_b[0:3, :], b1_rows[:, bass.ds(e, 1), c * F:(c + 1) * F], start=True, stop=False)
                    last = pe.matmul(o, fxT[:, k, :], w_1[:, bass.ds(e, 1), c * F:(c + 1) * F], start=False, stop=True)
                last.then_inc(up_psum, 1)

            def flip(t, k):
                pe.wait_ge(hid_ready, t + 1)
                need(pe, ht_ready, t)
                for f in range(FB):
                    last = pe.transpose(psQ[:, f * P:(f + 1) * P], hid[:, k, f * P:(f + 1) * P], ident[:, :])
                last.then_inc(ht_psum, 1)

            def down(t, k):
                e = pe.value_load(tile_expert[0:1, bass.ds(t, 1)], min_val=0, max_val=E - 1)
                pe.wait_ge(ht_ready, t + 1)
                need(pe, yb_ready, t)
                for f in range(FB):
                    last = pe.matmul(psO[:, 0:D], hT[:, k, f * P:(f + 1) * P],
                                     w_2[:, bass.ds(e, 1), f:f + 1, :], start=(f == 0), stop=(f == FB - 1))
                last.then_inc(y_psum, 1)

            turn(0, 0)
            up(0, 0)
            turn(0, 1)

            def tile(u, j):
                t, k = NR * u + j, j % 2
                inside = not isinstance(t, int)
                if inside or t + 1 < FT:
                    up(t + 1, 1 - k)
                flip(t, k)
                if inside or t + 2 < FT:
                    turn(u, j + 2)
                if inside or t > 0:
                    down(t - 1, 1 - k)

            for j in range(NR):
                tile(0, j)
            with pe.Fori(1, FT // NR) as u:
                for j in range(NR):
                    tile(u, j)
            for j in range(FT % NR):
                tile(FT // NR, j)
            down(FT - 1, (FT - 1) % 2)


_INS = ['x', 'ctx_1024', 'mask_1x1xSxS2_ik0', 'g_xattn', 'g_ffn', 'L0_xattn_wq', 'L0_xattn_bq', 'L0_xattn_wk',
        'L0_xattn_bk', 'L0_xattn_wv', 'L0_xattn_bv', 'L0_xattn_wo', 'L0_xattn_bo', 'L0_ffn_router_w',
        'L0_ffn_router_b', 'L0_ffn_w1', 'L0_ffn_b1', 'L0_ffn_w2', 'L0_ffn_b2']


def kernel(**inputs):
    import numpy as _np
    import concourse.bacc as _bacc
    from concourse import mybir as _mybir
    from concourse.bass_utils import run_bass_kernel_spmd as _run

    nc = _bacc.Bacc("TRN2", target_bir_lowering=False, num_devices=1)
    arrays, args = {}, []
    for name in _INS:
        a = _np.ascontiguousarray(inputs[name])
        arrays[f"in_{name}_dram"] = a
        args.append(nc.dram_tensor(f"in_{name}_dram", a.shape, _mybir.dt.from_np(a.dtype), kind="ExternalInput").ap())
    shape = inputs['x'].shape
    out = nc.dram_tensor("out_0_dram", shape, _mybir.dt.float32, kind="ExternalOutput").ap()
    gated_xattn_moe(nc, *args, out)
    r = _run(nc, [arrays], core_ids=[0])
    return r.results[0]["out_0_dram"]
```
